# Optimizing a Trainium2 kernel written in Bass

```python
import numpy as np
import jax
import jax.numpy as jnp

def _softmax(x, axis=-1):
    return jax.nn.softmax(x, axis=axis)

def _gelu(x):
    return jax.nn.gelu(x, approximate=True)

def _silu(x):
    return jax.nn.silu(x)

def _sigmoid(x):
    return jax.nn.sigmoid(x)

def _layernorm(x, axis=-1, eps=1e-05):
    m = jnp.mean(x, axis=axis, keepdims=True)
    v = jnp.var(x, axis=axis, keepdims=True)
    return (x - m) / jnp.sqrt(v + eps)

def _scatter_add(tgt, idx, src, axis=0):
    return tgt.at[idx].add(src)

def _segment_sum(src, seg, n):
    return jax.ops.segment_sum(src, seg, n)
kernel_name = 'mk_macaron_d1_jaxref_r8_82bf64'

def setup_inputs(seed: int=0):
    np.random.seed(seed)
    _w = jnp.asarray

    def _L0_attn_setup():
        import jax, jax.numpy as jnp
        import numpy as np
        GAMMA = 0.96875
        H = 128
        B = 4
        L = 256
        key = jax.random.key(seed)
        k0, k1, k2, k3, k4 = jax.random.split(key, 5)
        x = jax.random.normal(k0, (B, L, H), dtype=jnp.float32)
        weight_q = jax.random.normal(k1, (H, H), dtype=jnp.float32) / H
        weight_k = jax.random.normal(k2, (H, H), dtype=jnp.float32) / H
        weight_v = jax.random.normal(k3, (H, H), dtype=jnp.float32) / H
        theta = jax.random.normal(k4, (H,), dtype=jnp.float32) / H
        return {'x': x, 'weight_q': weight_q, 'weight_k': weight_k, 'weight_v': weight_v, 'theta': theta}
    _L0_attn_in = _L0_attn_setup()

    def _L0_ffn_setup():
        import jax, jax.numpy as jnp
        import numpy as np
        B, S, D, H, E, F, K = (2, 128, 128, 16, 8, 512, 2)
        EPS = 1e-05

        def _layernorm(x, g, b):
            mu = jnp.mean(x, axis=-1, keepdims=True)
            var = jnp.mean(jnp.square(x - mu), axis=-1, keepdims=True)
            return (x - mu) * jax.lax.rsqrt(var + EPS) * g + b
        key = jax.random.key(seed)
        ks = jax.random.split(key, 12)
        w = lambda k, shape: jax.random.normal(k, shape, dtype=jnp.float32) * 0.02
        return {'x': jax.random.normal(ks[0], (B, S, D), dtype=jnp.float32), 'ln1_g': jnp.ones((D,), jnp.float32), 'ln1_b': jnp.zeros((D,), jnp.float32), 'ln2_g': jnp.ones((D,), jnp.float32), 'ln2_b': jnp.zeros((D,), jnp.float32), 'Wq': w(ks[1], (D, D)), 'Wk': w(ks[2], (D, D)), 'Wv': w(ks[3], (D, D)), 'Wo': w(ks[4], (D, D)), 'Wg': w(ks[5], (D, E)), 'W1': w(ks[6], (E, D, F)), 'b1': jnp.zeros((E, F), jnp.float32), 'W2': w(ks[7], (E, F, D)), 'b2': jnp.zeros((E, D), jnp.float32)}
    _L0_ffn_in = _L0_ffn_setup()
    _d = {'L0_attn_x': _L0_attn_in['x'], 'L0_attn_weight_q': _L0_attn_in['weight_q'], 'L0_attn_weight_k': _L0_attn_in['weight_k'], 'L0_attn_weight_v': _L0_attn_in['weight_v'], 'L0_attn_theta': _L0_attn_in['theta'], 'L0_ffn_ln1_g': _L0_ffn_in['ln1_g'], 'L0_ffn_ln1_b': _L0_ffn_in['ln1_b'], 'L0_ffn_ln2_g': _L0_ffn_in['ln2_g'], 'L0_ffn_ln2_b': _L0_ffn_in['ln2_b'], 'L0_ffn_Wq': _L0_ffn_in['Wq'], 'L0_ffn_Wk': _L0_ffn_in['Wk'], 'L0_ffn_Wv': _L0_ffn_in['Wv'], 'L0_ffn_Wo': _L0_ffn_in['Wo'], 'L0_ffn_Wg': _L0_ffn_in['Wg'], 'L0_ffn_W1': _L0_ffn_in['W1'], 'L0_ffn_b1': _L0_ffn_in['b1'], 'L0_ffn_W2': _L0_ffn_in['W2'], 'L0_ffn_b2': _L0_ffn_in['b2']}
    _x0 = _d['L0_attn_x']
    _d['L0_attn_x'] = jax.random.normal(jax.random.fold_in(jax.random.key(seed), 1), (4, 1024, 128), dtype=_x0.dtype)
    del _x0
    return _d

def reference(L0_attn_x, L0_attn_weight_q, L0_attn_weight_k, L0_attn_weight_v, L0_attn_theta, L0_ffn_ln1_g, L0_ffn_ln1_b, L0_ffn_ln2_g, L0_ffn_ln2_b, L0_ffn_Wq, L0_ffn_Wk, L0_ffn_Wv, L0_ffn_Wo, L0_ffn_Wg, L0_ffn_W1, L0_ffn_b1, L0_ffn_W2, L0_ffn_b2):

    def _L0_attn_ref(x, weight_q, weight_k, weight_v, theta):
        import jax, jax.numpy as jnp
        import numpy as np
        GAMMA = 0.96875
        H = 128
        B = 4
        L = 256
        Bb, Ll, Hh = x.shape
        dt = x.dtype
        seq = jnp.arange(1, Ll + 1, dtype=dt)
        zero = jnp.asarray(0.0, dtype=dt)
        thetas = jnp.exp(zero * seq[:, None] * theta[None, :])
        theta_conj = thetas
        q = jnp.matmul(x, weight_q) * thetas[None]
        k = jnp.matmul(x, weight_k) * theta_conj[None]
        v = jnp.matmul(x, weight_v)
        n = jnp.arange(Ll)
        diff = n[:, None] - n[None, :]
        D = jnp.where(diff >= 0, jnp.asarray(GAMMA, dt) ** diff.astype(dt), jnp.zeros((), dt))
        scores = jnp.einsum('bid,bjd->bij', q, k) * D[None]
        return jnp.einsum('bij,bjd->bid', scores, v)

    def _L0_ffn_ref(x, ln1_g, ln1_b, ln2_g, ln2_b, Wq, Wk, Wv, Wo, Wg, W1, b1, W2, b2):
        import jax, jax.numpy as jnp
        import numpy as np
        B, S, D, H, E, F, K = (2, 128, 128, 16, 8, 512, 2)
        EPS = 1e-05

        def _layernorm(x, g, b):
            mu = jnp.mean(x, axis=-1, keepdims=True)
            var = jnp.mean(jnp.square(x - mu), axis=-1, keepdims=True)
            return (x - mu) * jax.lax.rsqrt(var + EPS) * g + b
        Bb, Ss, Dd = x.shape
        Dh = Dd // H
        h = _layernorm(x, ln1_g, ln1_b)
        q = (h @ Wq).reshape(Bb, Ss, H, Dh)
        k = (h @ Wk).reshape(Bb, Ss, H, Dh)
        v = (h @ Wv).reshape(Bb, Ss, H, Dh)
        scores = jnp.einsum('bqhd,bkhd->bhqk', q, k) / jnp.sqrt(jnp.float32(Dh))
        attn = jax.nn.softmax(scores, axis=-1)
        ctx = jnp.einsum('bhqk,bkhd->bqhd', attn, v).reshape(Bb, Ss, Dd)
        x = x + ctx @ Wo
        m = _layernorm(x, ln2_g, ln2_b)
        xt = m.reshape(-1, Dd)
        T = xt.shape[0]
        probs = jax.nn.softmax(xt @ Wg, axis=-1)
        wts, idx = jax.lax.top_k(probs, K)
        wts = wts / jnp.sum(wts, axis=-1, keepdims=True)
        h1 = jax.nn.gelu(jnp.einsum('td,edf->etf', xt, W1) + b1[:, None, :])
        ye = jnp.einsum('etf,efd->etd', h1, W2) + b2[:, None, :]
        sel = ye[idx, jnp.arange(T)[:, None], :]
        moe_out = jnp.sum(wts[..., None] * sel, axis=1).reshape(Bb, Ss, Dd)
        return x + moe_out
    x = L0_attn_x
    x = x + 0.5 * _L0_ffn_ref(_layernorm(x, axis=-1), L0_ffn_ln1_g, L0_ffn_ln1_b, L0_ffn_ln2_g, L0_ffn_ln2_b, L0_ffn_Wq, L0_ffn_Wk, L0_ffn_Wv, L0_ffn_Wo, L0_ffn_Wg, L0_ffn_W1, L0_ffn_b1, L0_ffn_W2, L0_ffn_b2)
    x = x + _L0_attn_ref(_layernorm(x, axis=-1), L0_attn_weight_q, L0_attn_weight_k, L0_attn_weight_v, L0_attn_theta)
    x = x + 0.5 * _L0_ffn_ref(_layernorm(x, axis=-1), L0_ffn_ln1_g, L0_ffn_ln1_b, L0_ffn_ln2_g, L0_ffn_ln2_b, L0_ffn_Wq, L0_ffn_Wk, L0_ffn_Wv, L0_ffn_Wo, L0_ffn_Wg, L0_ffn_W1, L0_ffn_b1, L0_ffn_W2, L0_ffn_b2)
    return x

_drawn_inputs = setup_inputs


def setup_inputs(seed=0):
    import zlib

    import numpy as np

    out = dict(_drawn_inputs(seed))
    spreads = {'L0_ffn_ln1_g': (1.0, 0.6),
     'L0_ffn_ln1_b': (0.0, 0.8),
     'L0_ffn_ln2_g': (1.0, 0.6),
     'L0_ffn_ln2_b': (0.0, 0.737),
     'L0_ffn_b1': (0.0, 0.799),
     'L0_ffn_b2': (0.0, 0.444)}
    factors = {'L0_ffn_Wq': 8.0, 'L0_ffn_Wk': 8.0, 'L0_ffn_Wv': 8.0, 'L0_ffn_Wo': 8.0, 'L0_ffn_W1': 3.011}
    for name, (base, spread) in spreads.items():
        noise = np.random.default_rng([zlib.crc32(name.encode()), seed]).standard_normal(out[name].shape)
        drawn = base * np.exp(spread * noise) if base else spread * noise
        out[name] = jnp.asarray(drawn.astype(out[name].dtype))
    for name, factor in factors.items():
        out[name] = (out[name] * factor).astype(out[name].dtype)
    return out
```

```python
from contextlib import ExitStack

import concourse.bass as bass
from concourse import mybir

ALU = mybir.AluOpType
ACT = mybir.ActivationFunctionType
F32 = mybir.dt.float32
BF16 = mybir.dt.bfloat16
AX = mybir.AxisListType

P = 128
D = 128
BATCH, SEQ = 4, 1024
TOK = BATCH * SEQ
TILES = TOK // P
CHUNKS = TILES // 4
HEADS, DH = 16, 8
GH = 4
GROUPS = BATCH * HEADS // GH
KT = SEQ // P
ROWS = 64
EXPERTS, FF = 8, 512
FB = FF // P
EPS = 1e-5
SCALE = float(DH) ** -0.5
GAMMA = 0.96875
Q_PARTS = (0, 0, 1, 1, 0, 2)
K_PARTS = (0, 1, 0, 1, 2, 0)
MAX_ROW = 8 * len(Q_PARTS)
C_IDENT, C_MASK, C_ROW, C_COL, C_RANK, C_END = 0, 128, 256, 384, 385, 393

SMALL = (("table", C_END), ("cols", 8), ("wqkv", 3 * D), ("wo", D), ("wg", EXPERTS), ("rw", 4 * D),
         ("b1", EXPERTS * FB), ("b2", EXPERTS))

TURNS = (("k_late", 0), ("ctx1", 2), ("q_late", 4), ("qm_late", 6), ("ctx0", 10), ("qm_early", 11),
         ("k_early", 13), ("q_early", 14))


def turns(g):
    there = {"k_late": 0 <= g + 1 < GROUPS, "ctx1": 0 <= g - 1, "q_late": 0 <= g + 1 < GROUPS,
             "qm_late": 0 <= g < GROUPS, "ctx0": 0 <= g < GROUPS, "qm_early": 0 <= g + 1 < GROUPS,
             "k_early": 0 <= g + 2 < GROUPS, "q_early": 0 <= g + 2 < GROUPS}
    return [(name, s) for name, s in TURNS if there[name]]


BODIES = list(range(-2, GROUPS + 1))
TURNS_OF_LAYER = sum(len(turns(g)) for g in BODIES)
FULL = len(TURNS)
LOOPED = (1, 13)


def turns_before(g):
    if isinstance(g, int):
        return sum(len(turns(i)) for i in BODIES if i < g)
    return g * FULL + (turns_before(1) - FULL)


def bodies(eng, emit):
    for g in (-2, -1, 0):
        emit(g, g % 2, g)
    with eng.Fori(0, (LOOPED[1] - LOOPED[0]) // 2) as i:
        emit(i * 2 + 1, 1, 1)
        emit(i * 2 + 2, 0, 2)
    for g in range(LOOPED[1], GROUPS + 1):
        emit(g, g % 2, g)


class Chain:

    def __init__(self, eng, sem, apart=None):
        self.eng, self.sem, self.n, self.base, self.apart = eng, sem, 0, 0, apart

    def link(self, ins):
        self.n += 1
        ins.then_inc(self.sem, 1)
        self.eng.wait_ge(self.sem, self.base + self.n)
        if self.apart and not isinstance(self.base, int):
            self.apart()

    def loop(self, i, per):
        self.start = self.n
        self.base = i * per

    def end(self, times, per):
        assert self.n == self.start + per, (self.n - self.start, per)
        self.n = self.start + times * per
        self.base = 0


def macaron(nc, x_in, small_in, w1, w2, out):
    with ExitStack() as ctx:
        def sb(name, shape, dt=F32):
            return ctx.enter_context(nc.sbuf_tensor(name, shape, dt))

        def sem(name):
            return ctx.enter_context(nc.semaphore(name))

        x = sb("x", [P, TILES * D])
        y = sb("y", [P, TILES * D])
        qkv = sb("qkv", [P, 3 * TILES * D])
        cx = sb("cx", [P, TILES * D])
        w1_sb = sb("w1_sb", [P, EXPERTS, FF])
        w2_sb = sb("w2_sb", [P, EXPERTS, FB, D])
        small = sb("small", [P, sum(w for _, w in SMALL)])
        at = dict(zip([name for name, _ in SMALL], [sum(w for _, w in SMALL[:i]) for i in range(len(SMALL))]))
        part = {name: small[:, at[name]:at[name] + w] for name, w in SMALL}
        wqkv_sb, wo_sb, wg_sb, rw_sb, b2_sb, tab = (part[n] for n in ("wqkv", "wo", "wg", "rw", "b2", "table"))
        b1_sb = part["b1"].rearrange("p (e f) -> p e f", e=EXPERTS)
        cols = part["cols"]
        ident_b = sb("ident_b", [P, P], BF16)
        st = sb("st", [P, TILES * 6])
        mean = sb("mean", [P, TILES])
        var = sb("var", [P, TILES])
        rstd = sb("rstd", [P, TILES])
        rstd2 = sb("rstd2", [P, TILES])
        shift = sb("shift", [P, TILES])
        sd = sb("sd", [P, TILES])
        ta = sb("ta", [P, TILES])
        tb = sb("tb", [P, TILES])
        kst = sb("kst", [P, KT, GH, ROWS], BF16)
        qst = [sb(f"qst{i}", [P, KT, GH, ROWS], BF16) for i in range(2)]
        vst = [sb(f"vst{i}", [P, KT, GH, 32]) for i in range(2)]
        kpad = [sb(f"kpad{i}", [P, GH, SEQ], BF16) for i in range(2)]
        q0 = [sb(f"q0{i}", [P, 2, 512], BF16) for i in range(2)]
        qm = [sb(f"qm{i}", [P, 2, 512], BF16) for i in range(2)]
        pbuf = sb("pbuf", [P, 2, GH, 512])
        ct = sb("ct", [P, 512])
        rest = sb("rest", [P, 2, KT * GH * DH])
        nmax = sb("nmax", [P, 2, 2, 16])
        negm = sb("negm", [P, 16])
        negr = sb("negr", [P, 16])
        rden = sb("rden", [P, 16])
        zn = [pbuf[:, 0, 0, :], pbuf[:, 0, 1, :]]
        ht = [pbuf[:, 0, 2, :], pbuf[:, 0, 3, :]]
        wbc = [qkv[:, 4096 * i:4096 * (i + 1)] for i in range(2)]
        h1 = [qkv[:, 8192 + 512 * i:8704 + 512 * i] for i in range(4)]
        acc = qkv[:, 10240:10752]
        mt = [qkv[:, 10752 + 512 * i:11264 + 512 * i] for i in range(2)]
        cbuf = pbuf[:, 0, 0, :]
        cxt = pbuf[:, 0, 1, :]
        x2 = pbuf[:, 0, 2, :]
        zn2 = pbuf[:, 0, 3, :]
        tmp = [pbuf[:, 1, 0, :], pbuf[:, 1, 1, :]]
        wts_t = pbuf[0:32, 1, 2, 0:128]
        gate = sb("gate", [P, 8, 32])
        gs = sb("gs", [P, 8, 4])
        st2 = sb("st2", [P, 4, 6])
        mv2 = sb("mv2", [P, 4, 2])
        ln2c = sb("ln2c", [P, 4, 4])
        rzt, rq, rk, rqd = pbuf[:, 1, 0, :], pbuf[:, 1, 1, :], pbuf[:, 1, 2, :], pbuf[:, 1, 3, :]
        rv, rkd, ram = qkv[:, 0:512], qkv[:, 512:1024], qkv[:, 1024:1536]
        state = sb("state", [P, BATCH * D])
        w_dram = nc.dram_tensor("w_scratch", [2, 32, P], F32, kind="Internal").ap()

        ps = ctx.enter_context(nc.psum_tensor("ps", [P, 8, 512], F32))

        ident = tab[:, C_IDENT:C_IDENT + P]
        qkv5 = qkv[:, :].rearrange("p (a h n) -> p a h n", a=3, h=4)

        x_loaded, w_loaded = sem("x_loaded"), sem("w_loaded")
        consts_done, ones_done, theta_z, theta_e = (sem("consts_done"), sem("ones_done"), sem("theta_z"),
                                                    sem("theta_e"))
        stats_done, var_ready, sd_ready, norm_ready = (sem("stats_done"), sem("var_ready"),
                                                       sem("sd_ready"), sem("norm_ready"))
        dve_seq, pool_seq = sem("dve_seq"), sem("pool_seq")
        zn_ready, zn_turned, ht_ready, qkv_done, qkv_stored, y_stored = (
            sem("zn_ready"), sem("zn_turned"), sem("ht_ready"), sem("qkv_done"), sem("qkv_stored"),
            sem("y_stored"))
        kst_ready, qst_ready, vst_ready = sem("kst_ready"), sem("qst_ready"), sem("vst_ready")
        turned, turn_taken = sem("turned"), sem("turn_taken")
        max_filled, max_taken = sem("max_filled"), sem("max_taken")
        neg_ready = sem("neg_ready")
        s_filled, exp_done, pv_done, ct_ready = sem("s_filled"), sem("exp_done"), sem("pv_done"), sem("ct_ready")
        cbuf_ready, cx_turned, cxt_ready, wo_done, x2_ready, var2_ready, sd2_ready, norm2_ready = (
            sem("cbuf_ready"), sem("cx_turned"), sem("cxt_ready"), sem("wo_done"), sem("x2_ready"),
            sem("var2_ready"), sem("sd2_ready"), sem("norm2_ready"))
        zn2_ready, zn2_turned, mt_ready, logits_done, lm_ready, ex_ready, w_ready, w_turned, wt_ready = (
            sem("zn2_ready"), sem("zn2_turned"), sem("mt_ready"), sem("logits_done"), sem("lm_ready"),
            sem("ex_ready"), sem("w_ready"), sem("w_turned"), sem("wt_ready"))
        w_written, w_spread = sem("w_written"), sem("w_spread")
        h_filled, gelu_done, y_filled, tmp_ready, tmp_added, out_turned, x_final = (
            sem("h_filled"), sem("gelu_done"), sem("y_filled"), sem("tmp_ready"), sem("tmp_added"),
            sem("out_turned"), sem("x_final"))
        rz_ready, rz_turned, rzt_ready, rq_done, rk_done, rkv_done, rq_ready, rk_ready = (
            sem("rz_ready"), sem("rz_turned"), sem("rzt_ready"), sem("rq_done"), sem("rk_done"),
            sem("rkv_done"), sem("rq_ready"), sem("rk_ready"))
        rkd_ready, rv_ready, rqd_ready, ra_done, ram_ready, ro_done, rst_done, rx_done, state_ready = (
            sem("rkd_ready"), sem("rv_ready"), sem("rqd_ready"), sem("ra_done"), sem("ram_ready"),
            sem("ro_done"), sem("rst_done"), sem("rx_done"), sem("state_ready"))
        stored = sem("stored")

        W_DMAS = 3

        block = ctx.enter_context(nc.Block())

        @block.sync
        def _(sp):
            sp.dma_start(small[:, :], small_in).then_inc(w_loaded, 16)
            for i in range(4):
                cut = slice(i * 1024, (i + 1) * 1024)
                sp.dma_start(x[:, cut], x_in[:, cut]).then_inc(x_loaded, 16)
            sp.dma_start(w1_sb[:, :, :], w1).then_inc(w_loaded, 16)
            sp.dma_start(w2_sb[:, :, :, :], w2).then_inc(w_loaded, 16)

            def spread(layer, c, par):
                n = layer * CHUNKS + c
                sp.wait_ge(wt_ready, n + 1)
                sp.dma_start(w_dram[par], wts_t).then_inc(w_written, 16)
                sp.wait_ge(w_written, n * 16 + 16)
                if par is not None and not (isinstance(c, int) and layer == 0 and c < 2):
                    sp.wait_ge(tmp_ready, n * 8 - 8)
                sp.dma_start(wbc[par], w_dram[par].rearrange("r t -> (r t)").partition_broadcast(P)
                             ).then_inc(w_spread, 16)

            def store(c):
                sp.wait_ge(x_final, CHUNKS + c + 1)
                cut = bass.ds(c * 512, 512)
                sp.dma_start(out[:, cut], x[:, cut]).then_inc(stored, 16)

            for layer in range(2):
                spread(layer, 0, 0)
                spread(layer, 1, 1)
                with sp.Fori(1, 4) as i:
                    for u in range(2):
                        if layer == 1:
                            store(i * 2 + (u - 2))
                        spread(layer, i * 2 + u, u)
            store(6)
            store(7)
            sp.wait_ge(stored, 16 * CHUNKS)

        @block.gpsimd
        def _(pool):
            def apart():
                pool.nop(nofuse=True)

            chain = Chain(pool, pool_seq, apart)
            for i in range(2):
                pool.memset(kpad[i][:, :, :], 0.0)
                pool.memset(vst[i][:, :, :, :], 0.0)
                pool.memset(qst[i][:, :, :, :], 0.0)
            pool.memset(state[:, :], 0.0)
            chain.link(pool.memset(kst[:, :, :, :], 0.0))
            pool.memset(kst[:, :, :, MAX_ROW:MAX_ROW + 3], 1.0)
            for i in range(2):
                last = pool.memset(vst[i][:, :, :, DH:DH + 1], 1.0)
            last.then_inc(ones_done, 1)

            def group_view(a, g):
                return qkv[:, bass.ds(g * 256 + a * TILES * D, 256)].rearrange(
                    "p (t h d) -> p t h d", t=KT, h=GH)

            def parts(a, g, dst, order):
                src = group_view(a, g)
                r = [rest[:, i, :].rearrange("p (t h d) -> p t h d", t=KT, h=GH) for i in range(2)]

                def rows(j):
                    return dst[:, :, :, 8 * j:8 * j + 8]

                level = [[j for j, part in enumerate(order) if part == n] for n in range(3)]
                for j in level[0][1:]:
                    pool.tensor_copy(rows(j), src)
                chain.link(pool.tensor_copy(rows(level[0][0]), src))
                chain.link(pool.tensor_tensor(r[0], src, rows(level[0][0]), ALU.subtract))
                for j in level[1][1:]:
                    pool.tensor_copy(rows(j), r[0])
                chain.link(pool.tensor_copy(rows(level[1][0]), r[0]))
                chain.link(pool.tensor_tensor(r[1], r[0], rows(level[1][0]), ALU.subtract))
                return pool.tensor_copy(rows(level[2][0]), r[1])

            def body(layer, g, par, n):
                at = dict((name, i) for i, (name, _) in enumerate(turns(n)))
                before = turns_before(g) + layer * TURNS_OF_LAYER
                G = g + layer * GROUPS
                if 0 <= n + 1 < GROUPS:
                    if n >= 1 or layer:
                        pool.wait_ge(ct_ready, G * 2)
                        apart()
                    pool.tensor_copy(vst[(par + 1) % 2][:, :, :, 0:DH],
                                     group_view(2, g + 1)).then_inc(vst_ready, 1)
                if 0 <= n + 2 < GROUPS:
                    if n >= -1:
                        pool.wait_ge(turned, before + at["k_late"] + 1)
                        apart()
                    parts(1, g + 2, kst, K_PARTS).then_inc(kst_ready, 1)
                    if n >= 0:
                        pool.wait_ge(turned, before + at["qm_late"] + 1)
                        apart()
                    chain.link(pool.memset(qst[par][:, :, :, MAX_ROW:MAX_ROW + 3], 0.0))
                    parts(0, g + 2, qst[par], Q_PARTS).then_inc(qst_ready, 1)

            def attend(layer):
                pool.wait_ge(qkv_stored, (layer + 1) * TILES)
                body(layer, -2, 0, -2)
                body(layer, -1, 1, -1)
                body(layer, 0, 0, 0)
                with pool.Fori(0, 6) as i:
                    chain.loop(i, 18)
                    body(layer, i * 2 + 1, 1, 1)
                    body(layer, i * 2 + 2, 0, 2)
                    chain.end(6, 18)
                for g in range(13, GROUPS + 1):
                    body(layer, g, g % 2, g)

            def gather_cx(layer, c):
                n = layer * CHUNKS + c
                if not isinstance(c, int) or c or layer:
                    pool.wait_ge(cx_turned, n)
                    apart()
                pool.tensor_copy(cbuf.rearrange("p (t h n) -> p h t n", t=4, h=4),
                                 cx[:, :].rearrange("p (h n) -> p h n", h=4)[:, :, bass.ds(c * 128, 128)]
                                 .rearrange("p h (t n) -> p h t n", t=4)).then_inc(cbuf_ready, 1)

            def sum_experts(layer, c):
                n = layer * CHUNKS + c
                first = isinstance(c, int) and c == 0 and layer == 0
                for e in range(1, EXPERTS):
                    pool.wait_ge(tmp_ready, n * 8 + e + 1)
                    if e == 1:
                        if not first:
                            pool.wait_ge(out_turned, n)
                        ins = pool.tensor_tensor(acc, tmp[0], tmp[1], ALU.add)
                    else:
                        pool.wait_ge(tmp_added, n * 7 + e - 1)
                        ins = pool.tensor_tensor(acc, acc, tmp[e % 2], ALU.add)
                    ins.then_inc(tmp_added, 1)

            def mix(layer):
                pool.wait_ge(turn_taken, (layer + 1) * TURNS_OF_LAYER)
                gather_cx(layer, 0)
                gather_cx(layer, 1)
                sum_experts(layer, 0)
                with pool.Fori(1, 7) as c:
                    gather_cx(layer, c + 1)
                    sum_experts(layer, c)
                sum_experts(layer, 7)

            def retain():
                with pool.Fori(0, KT) as c:
                    pool.wait_ge(rq_ready, c + 1)
                    pool.tensor_tensor(rqd.rearrange("p (b t) -> p b t", b=BATCH),
                                       rq.rearrange("p (b t) -> p b t", b=BATCH),
                                       tab[:, C_ROW:C_ROW + P].unsqueeze(1).broadcast_to([P, BATCH, P]),
                                       ALU.mult).then_inc(rqd_ready, 1)

            pool.wait_ge(w_loaded, 16 * W_DMAS)
            for layer in range(2):
                attend(layer)
                mix(layer)
                if layer == 0:
                    retain()

        @block.scalar
        def _(act):
            def std(n):
                act.wait_ge(var_ready, n)
                act.activation(sd[:, :], ta[:, :], ACT.Sqrt).then_inc(sd_ready, 1)

            def normed(dst, c, n):
                if not isinstance(c, int) or n > 1:
                    act.wait_ge(zn_turned, n - 1)
                for j in range(4):
                    t = c * 4 + j
                    last = act.activation(dst[:, j * D:(j + 1) * D], x[:, bass.ds(t * D, D)], ACT.Identity,
                                          scale=rstd2[:, bass.ds(t, 1)], bias=shift[:, bass.ds(t, 1)])
                last.then_inc(zn_ready, 1)

            def keep_qkv(layer, c):
                for j in range(4):
                    t = c * 4 + j
                    act.wait_ge(qkv_done, layer * TILES + t + 1)
                    act.activation(qkv5[:, :, :, bass.ds(t * 32, 32)],
                                   ps[:, j, 0:3 * D].rearrange("p (a h n) -> p a h n", a=3, h=4),
                                   ACT.Copy).then_inc(qkv_stored, 1)

            def project(layer):
                n = layer * CHUNKS
                std(3 * layer + 1)
                std(3 * layer + 2)
                act.wait_ge(norm_ready, 2 * layer + 1)
                normed(zn[0], 0, n)
                normed(zn[1], 1, n + 1)
                with act.Fori(0, 3) as i:
                    for u in range(2):
                        keep_qkv(layer, i * 2 + u)
                        normed(zn[u], i * 2 + (u + 2), i * 2 + (n + u + 2))
                keep_qkv(layer, 6)
                keep_qkv(layer, 7)

            def take_turn(name, par, count):
                act.wait_ge(turned, count)
                src = ps[:, 7, :].bitcast(BF16).rearrange("p (a n) -> p a n", a=2)
                if name in ("k_early", "k_late"):
                    kh = 512 * (name == "k_late")
                    k2 = (par + (name == "k_late")) % 2
                    for half in range(2):
                        rows = slice(64 * half, 64 * half + 64)
                        last = act.activation(kpad[k2][rows, half:GH:2, kh:kh + 512], src[rows, :, :], ACT.Copy)
                else:
                    dst = {"q_early": q0[0], "q_late": q0[1], "qm_early": qm[0], "qm_late": qm[1]}[name]
                    last = act.activation(dst[:, :, :], src, ACT.Copy)
                last.then_inc(turn_taken, 1)

            def body(layer, g, par, n):
                G = g + layer * GROUPS
                at = {s: (name, i) for i, (name, s) in enumerate(turns(n))}
                before = turns_before(g) + layer * TURNS_OF_LAYER
                for s in range(16 if n < GROUPS else 3):
                    if 0 <= n < GROUPS:
                        for u in range(GH):
                            act.wait_ge(s_filled, G * 64 + (4 * s + u + 1))
                            if u == 0 and (n > 0 or s > 1 or layer):
                                act.wait_ge(pv_done, G * 16 + (s - 1))
                            act.activation(pbuf[:, s % 2, u, :], ps[:, u % 2, :], ACT.Exp,
                                           scale=SCALE).then_inc(exp_done, 1)
                    if s in at and not at[s][0].startswith("ctx"):
                        take_turn(at[s][0], par, before + at[s][1] + 1)
                    if (s == 0 and n >= 1) or (s == 8 and 0 <= n < GROUPS):
                        act.wait_ge(pv_done, G * 16 + s)
                        act.activation(ct[:, :], ps[:, 6, :], ACT.Copy).then_inc(ct_ready, 1)

            def gelus(layer, c, after):
                n = layer * CHUNKS + c
                for k in range(32):
                    act.wait_ge(h_filled, n * 32 + (k + 1))
                    if k >= 4 or not (isinstance(c, int) and c == 0 and layer == 0):
                        act.wait_ge(y_filled, n * 8 + (k // 4))
                    act.activation(h1[k % 4], ps[:, k % 2, :], ACT.Gelu_apprx_tanh,
                                   bias=b1_sb[:, k // 4, k % 4:k % 4 + 1]).then_inc(gelu_done, 1)
                    for f in after.get(k, ()):
                        f()

            def chain_parts(layer, c, par):
                n = layer * CHUNKS + c

                def root():
                    act.wait_ge(var2_ready, n + 1)
                    act.activation(ln2c[:, 1, :], ln2c[:, 0, :], ACT.Sqrt).then_inc(sd2_ready, 1)

                def norm():
                    act.wait_ge(norm2_ready, n + 1)
                    for j in range(4):
                        last = act.activation(zn2[:, j * D:(j + 1) * D], x2[:, j * D:(j + 1) * D], ACT.Identity,
                                              scale=ln2c[:, 2, j:j + 1], bias=ln2c[:, 3, j:j + 1])
                    last.then_inc(zn2_ready, 1)

                def affine():
                    act.wait_ge(zn2_turned, n + 1)
                    act.activation(mt[par], ps[:, 5, :], ACT.Identity, scale=cols[:, 2:3],
                                   bias=cols[:, 3:4]).then_inc(mt_ready, 1)

                def expo():
                    act.wait_ge(lm_ready, n + 1)
                    act.activation(gate[:, 1, :], gate[:, 0, :], ACT.Exp).then_inc(ex_ready, 1)
                return root, norm, affine, expo

            def mix(layer):
                for f in chain_parts(layer, 0, 0):
                    f()

                def one(c, par):
                    root, norm, affine, expo = chain_parts(layer, c + 1, (par + 1) % 2)
                    gelus(layer, c, {6: (root,), 8: (norm,), 11: (affine,), 14: (expo,)})
                one(0, 0)
                with act.Fori(0, 3) as i:
                    one(i * 2 + 1, 1)
                    one(i * 2 + 2, 0)
                gelus(layer, 7, {})

            def retain():
                act.wait_ge(theta_z, 1)
                act.activation(cols[:, 6:7], cols[:, 5:6], ACT.Exp).then_inc(theta_e, 1)
                std(3)
                act.wait_ge(norm_ready, 2)
                act.wait_ge(theta_e, 2)

                def one(c, first):
                    if not first:
                        act.wait_ge(rz_turned, c)
                    for b in range(BATCH):
                        t = c + b * KT
                        last = act.activation(zn[0][:, b * D:(b + 1) * D], x[:, bass.ds(t * D, D)], ACT.Identity,
                                              scale=rstd[:, bass.ds(t, 1)], bias=shift[:, bass.ds(t, 1)])
                    last.then_inc(rz_ready, 1)
                    if not first:
                        act.wait_ge(rx_done, c)
                    act.wait_ge(rq_done, c + 1)
                    act.activation(rq, ps[:, 0, :], ACT.Copy, scale=cols[:, 7:8]).then_inc(rq_ready, 1)
                    act.wait_ge(rk_done, c + 1)
                    act.activation(rk, ps[:, 1, :], ACT.Copy).then_inc(rk_ready, 1)
                    act.wait_ge(rkv_done, c + 1)
                    act.activation(rkd.rearrange("p (b d) -> p b d", b=BATCH),
                                   ps[:, 2:4, :].rearrange("p a (b n) -> p (a b) n", b=2)[:, :, D:2 * D],
                                   ACT.Copy, scale=tab[:, C_COL:C_COL + 1]).then_inc(rkd_ready, 1)
                one(0, True)
                with act.Fori(1, KT) as c:
                    one(c, False)

            act.wait_ge(w_loaded, 16 * W_DMAS)
            act.wait_ge(ones_done, 1)
            for layer in range(2):
                project(layer)
                bodies(act, lambda g, par, n: body(layer, g, par, n))
                mix(layer)
                if layer == 0:
                    retain()

        @block.vector
        def _(dve):
            chain = Chain(dve, dve_seq)

            def stats(n):
                with dve.Fori(0, CHUNKS) as i:
                    for j in range(4):
                        dve.bn_stats(st[:, bass.ds(i * 24 + j * 6, 6)],
                                     x[:, bass.ds(i * 512 + j * D, D)]).then_inc(stats_done, 1)
                dve.wait_ge(stats_done, TILES * (n + 1))
                s = st[:, :].rearrange("p (t c) -> p t c", c=6)
                dve.tensor_tensor(ta[:, :], s[:, :, 1], s[:, :, 4], ALU.subtract)
                dve.tensor_tensor(tb[:, :], s[:, :, 2], s[:, :, 5], ALU.add)
                chain.link(dve.tensor_tensor(mean[:, :], s[:, :, 1], s[:, :, 4], ALU.add))
                dve.tensor_scalar(mean[:, :], mean[:, :], 0.5, None, ALU.mult)
                dve.tensor_scalar(tb[:, :], tb[:, :], 1.0 / D, None, ALU.mult)
                chain.link(dve.tensor_tensor(ta[:, :], ta[:, :], ta[:, :], ALU.mult))
                chain.link(dve.scalar_tensor_tensor(out=var[:, :], in0=ta[:, :], scalar=0.25, in1=tb[:, :],
                                                    op0=ALU.mult, op1=ALU.add))
                dve.tensor_scalar(ta[:, :], var[:, :], EPS, None, ALU.add).then_inc(var_ready, 1)

            def ht_evac(c, u, n):
                dve.wait_ge(zn_turned, n + 1)
                dve.tensor_scalar(ht[u], ps[:, 6 + u, :], cols[:, 0:1], cols[:, 1:2], ALU.mult,
                                  ALU.add).then_inc(ht_ready, 1)

            def project(layer):
                if layer == 0:
                    dve.wait_ge(x_loaded, 64)
                stats(2 * layer)
                dve.wait_ge(sd_ready, 3 * layer + 1)
                chain.link(dve.reciprocal(rstd[:, :], sd[:, :]))
                chain.link(dve.tensor_tensor(tb[:, :], rstd[:, :], rstd[:, :], ALU.mult))
                chain.link(dve.tensor_tensor(tb[:, :], tb[:, :], var[:, :], ALU.mult))
                dve.tensor_scalar(ta[:, :], tb[:, :], EPS, None, ALU.add).then_inc(var_ready, 1)
                dve.wait_ge(sd_ready, 3 * layer + 2)
                chain.link(dve.reciprocal(rstd2[:, :], sd[:, :]))
                chain.link(dve.tensor_tensor(rstd2[:, :], rstd2[:, :], rstd[:, :], ALU.mult))
                dve.scalar_tensor_tensor(out=shift[:, :], in0=mean[:, :], scalar=-1.0, in1=rstd2[:, :],
                                         op0=ALU.mult, op1=ALU.mult).then_inc(norm_ready, 1)
                with dve.Fori(0, CHUNKS // 2) as i:
                    for u in range(2):
                        for j in range(4):
                            t = i * 8 + (4 * u + j)
                            dve.tensor_scalar(y[:, bass.ds(t * D, D)], x[:, bass.ds(t * D, D)],
                                              mean[:, bass.ds(t, 1)], rstd[:, bass.ds(t, 1)],
                                              ALU.subtract, ALU.mult).then_inc(y_stored, 1)
                        ht_evac(i * 2 + u, u, i * 2 + (layer * CHUNKS + u))

            def neg_step(layer, g, par, half, k):
                col = qst[par][:, 4 * half:4 * half + 4, :, :]
                a = negm[:, :].rearrange("p (t h) -> p t h", t=4)
                r = negr[:, :].rearrange("p (t h) -> p t h", t=4)
                part = [col[:, :, :, MAX_ROW + i] for i in range(3)]
                if k == 0:
                    link = dve.tensor_tensor(negm[:, :], nmax[:, half, 0, :], nmax[:, half, 1, :], ALU.min)
                elif k == 1:
                    link = dve.tensor_copy(part[0], a)
                elif k == 2:
                    link = dve.tensor_tensor(r, a, part[0], ALU.subtract)
                elif k == 3:
                    link = dve.tensor_copy(part[1], r)
                elif k == 4:
                    link = dve.tensor_tensor(a, r, part[1], ALU.subtract)
                else:
                    dve.tensor_copy(part[2], a).then_inc(neg_ready, 1)
                    return
                chain.link(link)

            def body(layer, g, par, n):
                G = g + layer * GROUPS
                at = {s: (name, i) for i, (name, s) in enumerate(turns(n))}
                before = turns_before(g) + layer * TURNS_OF_LAYER
                for s in range(16 if n < GROUPS else 3):
                    half, kh, j = s // 8, s % 8 // 4, s % 4
                    if s == 0 and 0 <= n < GROUPS:
                        dve.wait_ge(max_taken, (G + 1) * 64)
                        for k in range(6):
                            neg_step(layer, g, par, 1, k)
                    if s == 8 and 0 <= n + 1 < GROUPS:
                        dve.wait_ge(max_taken, (G + 1) * 64 + 32)
                        for k in range(6):
                            neg_step(layer, g + 1, (par + 1) % 2, 0, k)
                    if 0 <= n + 1 < GROUPS:
                        for u in range(GH):
                            dve.wait_ge(max_filled, (G + 1) * 64 + (4 * s + u + 1))
                            dve.tensor_reduce(nmax[:, half, kh, 4 * j + u:4 * j + u + 1], ps[:, 2 + u, :],
                                              AX.X, ALU.max, negate=True).then_inc(max_taken, 1)
                    if s in at and at[s][0].startswith("ctx"):
                        name, i = at[s]
                        half_done = 1 if name == "ctx1" else 0
                        dve.wait_ge(turned, before + i + 1)
                        src = ps[:, 7, :].rearrange("p (t h n) -> p t h n", t=4, h=GH)
                        rd = rden[:, :].rearrange("p (t h) -> p t h", t=4)
                        chain.link(dve.reciprocal(rd, src[:, :, :, DH]))
                        g2 = g if name == "ctx0" else g - 1
                        dve.tensor_tensor(
                            cx[:, bass.ds(g2 * 256 + half_done * 128, 128)].rearrange(
                                "p (t h n) -> p t h n", t=4, h=GH),
                            src[:, :, :, 0:DH], rd.unsqueeze(3).broadcast_to([P, 4, GH, DH]),
                            ALU.mult).then_inc(turn_taken, 1)

            def attend(layer):
                for g in (-2, -1, 0):
                    body(layer, g, g % 2, g)
                with dve.Fori(0, 6) as i:
                    chain.loop(i, 24)
                    body(layer, i * 2 + 1, 1, 1)
                    body(layer, i * 2 + 2, 0, 2)
                    chain.end(6, 24)
                for g in range(13, GROUPS + 1):
                    body(layer, g, g % 2, g)

            g3 = [gate[:, i, :].rearrange("p (t e) -> p t e", t=4) for i in range(8)]
            rank = tab[:, C_RANK:C_RANK + EXPERTS].unsqueeze(1).broadcast_to([P, 4, EXPERTS])

            def bc(i):
                return gs[:, i, :].unsqueeze(2).broadcast_to([P, 4, EXPERTS])

            def chain_parts(layer, c):
                n = layer * CHUNKS + c

                def copy_cx():
                    dve.wait_ge(cx_turned, n + 1)
                    dve.tensor_copy(cxt, ps[:, 5, :]).then_inc(cxt_ready, 1)

                def residual():
                    dve.wait_ge(wo_done, n + 1)
                    if not (isinstance(c, int) and c == 0 and layer == 0):
                        dve.wait_ge(zn2_ready, n)
                    chain.link(dve.tensor_tensor(x2, ps[:, 4, :], y[:, bass.ds(c * 512, 512)], ALU.add))
                    for j in range(4):
                        last = dve.bn_stats(st2[:, j, :], x2[:, j * D:(j + 1) * D])
                    chain.link(last)
                    dve.nop(nofuse=True)
                    for j in range(4):
                        last = dve.bn_aggr(mv2[:, j, :], st2[:, j, :])
                    chain.link(last)
                    dve.tensor_scalar(ln2c[:, 0, :], mv2[:, :, 1], EPS, None, ALU.add).then_inc(var2_ready, 1)
                    xs = x[:, bass.ds(c * 512, 512)]
                    dve.scalar_tensor_tensor(out=xs, in0=x2, scalar=0.5, in1=xs, op0=ALU.mult,
                                             op1=ALU.add).then_inc(x2_ready, 1)

                def shift2():
                    dve.wait_ge(sd2_ready, n + 1)
                    chain.link(dve.reciprocal(ln2c[:, 2, :], ln2c[:, 1, :]))
                    dve.scalar_tensor_tensor(out=ln2c[:, 3, :], in0=mv2[:, :, 0], scalar=-1.0, in1=ln2c[:, 2, :],
                                             op0=ALU.mult, op1=ALU.mult).then_inc(norm2_ready, 1)

                def gate1():
                    dve.wait_ge(logits_done, n + 1)
                    lg = ps[:, 4, 0:32].rearrange("p (t e) -> p t e", t=4)
                    chain.link(dve.tensor_reduce(gs[:, 0, :], lg, AX.X, ALU.max))
                    dve.tensor_tensor(g3[0], lg, bc(0), ALU.subtract).then_inc(lm_ready, 1)

                def gate2():
                    dve.wait_ge(ex_ready, n + 1)
                    chain.link(dve.tensor_reduce(gs[:, 1, :], g3[1], AX.X, ALU.add))
                    chain.link(dve.reciprocal(gs[:, 1, :], gs[:, 1, :]))
                    chain.link(dve.tensor_tensor(g3[2], g3[1], bc(1), ALU.mult))

                    def top(src, value, onehot):
                        chain.link(dve.tensor_reduce(gs[:, value, :], src, AX.X, ALU.max))
                        chain.link(dve.tensor_tensor(g3[6], src, bc(value), ALU.is_equal))
                        chain.link(dve.tensor_tensor(g3[6], g3[6], rank, ALU.mult))
                        chain.link(dve.tensor_reduce(gs[:, 4, :], g3[6], AX.X, ALU.max))
                        chain.link(dve.tensor_tensor(g3[onehot], bc(4), rank, ALU.is_equal))
                    top(g3[2], 2, 3)
                    chain.link(dve.scalar_tensor_tensor(out=g3[4], in0=g3[3], scalar=-2.0, in1=g3[2],
                                                        op0=ALU.mult, op1=ALU.add))
                    top(g3[4], 3, 5)
                    dve.tensor_tensor(g3[3], g3[3], g3[5], ALU.add)
                    chain.link(dve.tensor_tensor(gs[:, 5, :], gs[:, 2, :], gs[:, 3, :], ALU.add))
                    chain.link(dve.reciprocal(gs[:, 5, :], gs[:, 5, :]))
                    chain.link(dve.tensor_tensor(g3[3], g3[3], g3[2], ALU.mult))
                    if not (isinstance(c, int) and c == 0 and layer == 0):
                        dve.wait_ge(w_turned, n)
                    dve.tensor_tensor(gate[:, 7, :].rearrange("p (e t) -> p t e", e=EXPERTS), g3[3], bc(5),
                                      ALU.mult).then_inc(w_ready, 1)

                def copy_w():
                    dve.wait_ge(w_turned, n + 1)
                    if not (isinstance(c, int) and c == 0 and layer == 0):
                        dve.wait_ge(w_written, n * 16)
                    dve.tensor_copy(wts_t, ps[0:32, 5, 0:128]).then_inc(wt_ready, 1)
                return copy_cx, residual, shift2, gate1, gate2, copy_w

            CHAIN_LINKS = 3 + 1 + 1 + 3 + 5 + 1 + 5 + 3

            def expert(layer, c, par, e):
                n = layer * CHUNKS + c
                first = isinstance(c, int) and c == 0 and layer == 0
                if e == 0:
                    dve.wait_ge(w_spread, n * 16 + 16)
                dve.wait_ge(y_filled, n * 8 + e + 1)
                if e == 0 or e == 1:
                    if not first:
                        dve.wait_ge(tmp_added, n * 7)
                else:
                    dve.wait_ge(tmp_added, n * 7 + e - 1)
                dve.scalar_tensor_tensor(out=tmp[e % 2], in0=ps[:, 2 + e % 2, :], scalar=b2_sb[:, e:e + 1],
                                         in1=wbc[par][:, e * 512:(e + 1) * 512], op0=ALU.add,
                                         op1=ALU.mult).then_inc(tmp_ready, 1)

            def finish(layer, c):
                n = layer * CHUNKS + c
                dve.wait_ge(out_turned, n + 1)
                xs = x[:, bass.ds(c * 512, 512)]
                dve.scalar_tensor_tensor(out=xs, in0=ps[:, 7, :], scalar=0.5, in1=xs, op0=ALU.mult,
                                         op1=ALU.add).then_inc(x_final, 1)

            def mix(layer):
                for f in chain_parts(layer, 0):
                    f()

                def one(c, par, before, after):
                    parts = chain_parts(layer, c + 1) if after else None
                    for e in range(EXPERTS):
                        if after and e == 0:
                            parts[0]()
                            parts[1]()
                        expert(layer, c, par, e)
                        if after and e == 0:
                            parts[2]()
                        if before and e == 1:
                            finish(layer, c - 1)
                        if after and e == 2:
                            parts[3]()
                        if after and e == 3:
                            parts[4]()
                        if after and e == 4:
                            parts[5]()
                one(0, 0, False, True)
                with dve.Fori(0, 3) as i:
                    chain.loop(i, 2 * CHAIN_LINKS)
                    one(i * 2 + 1, 1, True, True)
                    one(i * 2 + 2, 0, True, True)
                    chain.end(3, 2 * CHAIN_LINKS)
                one(7, 1, True, False)
                finish(layer, 7)

            def retain():
                chain.link(dve.tensor_scalar(cols[:, 5:6], cols[:, 4:5], 0.0, None, ALU.mult))
                dve.tensor_copy(cols[:, 5:6], cols[:, 5:6]).then_inc(theta_z, 1)
                dve.wait_ge(x_final, CHUNKS)
                stats(1)
                dve.wait_ge(sd_ready, 3)
                chain.link(dve.reciprocal(rstd[:, :], sd[:, :]))
                dve.scalar_tensor_tensor(out=shift[:, :], in0=mean[:, :], scalar=-1.0, in1=rstd[:, :],
                                         op0=ALU.mult, op1=ALU.mult).then_inc(norm_ready, 1)
                dve.wait_ge(theta_e, 1)
                dve.tensor_tensor(cols[:, 7:8], cols[:, 6:7], cols[:, 6:7], ALU.mult).then_inc(theta_e, 1)
                b4 = "p (b n) -> p b n"
                with dve.Fori(0, KT) as c:
                    dve.wait_ge(rz_turned, c + 1)
                    dve.tensor_copy(rzt, ps[:, 7, :]).then_inc(rzt_ready, 1)
                    dve.wait_ge(rkd_ready, c + 1)
                    dve.tensor_copy(rv.rearrange(b4, b=BATCH),
                                    ps[:, 2:4, :].rearrange("p a (b n) -> p (a b) n", b=2)[:, :, 0:D]
                                    ).then_inc(rv_ready, 1)
                    dve.wait_ge(ra_done, c + 1)
                    dve.tensor_tensor(ram.rearrange(b4, b=BATCH), ps[:, 4, :].rearrange(b4, b=BATCH),
                                      tab[:, C_MASK:C_MASK + P].unsqueeze(1).broadcast_to([P, BATCH, P]),
                                      ALU.mult).then_inc(ram_ready, 1)
                    dve.wait_ge(ro_done, c + 1)
                    xs = x[:, :].rearrange(b4, b=BATCH)[:, :, bass.ds(c * D, D)]
                    dve.tensor_tensor(xs, ps[:, 5, :].rearrange(b4, b=BATCH), xs, ALU.add).then_inc(rx_done, 1)
                    dve.wait_ge(rst_done, c + 1)
                    dve.scalar_tensor_tensor(out=state[:, :], in0=state[:, :], scalar=GAMMA ** P,
                                             in1=ps[:, 6, :], op0=ALU.mult, op1=ALU.add
                                             ).then_inc(state_ready, 1)
                dve.wait_ge(rx_done, KT)

            dve.wait_ge(w_loaded, 16 * W_DMAS)
            dve.tensor_copy(ident_b[:, :], ident).then_inc(consts_done, 1)
            for layer in range(2):
                project(layer)
                attend(layer)
                mix(layer)
                if layer == 0:
                    retain()

        @block.tensor
        def _(pe):
            mm = pe.matmul

            def turn4(bank, src):
                for j in range(4):
                    last = pe.transpose(ps[:, bank, j * P:(j + 1) * P], src[:, j * P:(j + 1) * P], ident)
                return last

            def project(layer):
                def one(c, u, n):
                    early = isinstance(c, int) and layer == 0
                    pe.wait_ge(zn_ready, n + 1)
                    if not early or c >= 2:
                        pe.wait_ge(ht_ready, n - 1)
                    turn4(6 + u, zn[u]).then_inc(zn_turned, 1)
                    pe.wait_ge(ht_ready, n + 1)
                    for j in range(4):
                        if not early or c >= 1:
                            pe.wait_ge(qkv_stored, n * 4 + (j - 3))
                        mm(ps[:, j, 0:3 * D], ht[u][:, j * P:(j + 1) * P], wqkv_sb[:, :], start=True,
                           stop=True).then_inc(qkv_done, 1)
                n = layer * CHUNKS
                one(0, 0, n)
                one(1, 1, n + 1)
                with pe.Fori(1, CHUNKS // 2) as i:
                    one(i * 2, 0, i * 2 + n)
                    one(i * 2 + 1, 1, i * 2 + (n + 1))

            def turn(layer, name, par, G, count, first):
                if not first:
                    pe.wait_ge(turn_taken, count)
                if name in ("ctx0", "ctx1"):
                    pe.wait_ge(ct_ready, G * 2 + (1 if name == "ctx0" else 0))
                    turn4(7, ct[:, :]).then_inc(turned, 1)
                    return
                if name in ("k_early", "q_early"):
                    pe.wait_ge(kst_ready if name == "k_early" else qst_ready, G + 3)
                if name == "qm_late":
                    pe.wait_ge(neg_ready, G * 2 + 2)
                if name == "qm_early":
                    pe.wait_ge(neg_ready, G * 2 + 3)
                src, half = {"k_late": (kst, 1), "k_early": (kst, 0), "q_late": (qst[(par + 1) % 2], 1),
                             "q_early": (qst[par], 0), "qm_late": (qst[par], 1),
                             "qm_early": (qst[(par + 1) % 2], 0)}[name]
                dst = ps[:, 7, :].bitcast(BF16).rearrange("p (a n) -> p a n", a=2)
                for pair in range(2):
                    for t in range(4):
                        last = pe.transpose(dst[:, pair, t * P:(t + 1) * P],
                                            src[:, 4 * half + t, 2 * pair:2 * pair + 2, :], ident_b[:, :])
                last.then_inc(turned, 1)

            def body(layer, g, par, n):
                G = g + layer * GROUPS
                at = {s: (name, i) for i, (name, s) in enumerate(turns(n))}
                before = turns_before(g) + layer * TURNS_OF_LAYER
                attends, takes_max = 0 <= n < GROUPS, 0 <= n + 1 < GROUPS

                def score(s, u):
                    if n or s or u > 1 or layer:
                        pe.wait_ge(exp_done, G * 64 + (4 * s + u - 1))
                    mm(ps[:, u % 2, :], kpad[par][:, u, s % 8 * P:(s % 8 + 1) * P], qm[s // 8][:, u // 2, :],
                       start=True, stop=True).then_inc(s_filled, 1)

                def top(s, u):
                    half, kh, j = s // 8, s % 8 // 4, s % 4
                    if n >= 0 or s or layer:
                        pe.wait_ge(max_taken, G * 64 + (64 + 4 * s + u - 3))
                    mm(ps[:, 2 + u, :], q0[half][:, u // 2, j * P:(j + 1) * P],
                       kpad[(par + 1) % 2][:, u, kh * 512:kh * 512 + 512], start=True,
                       stop=True).then_inc(max_filled, 1)

                def weigh(s, G, par):
                    pe.wait_ge(exp_done, G * 64 + (4 * s + 4))
                    if s == 0:
                        pe.wait_ge(vst_ready, G + 1)
                    if s % 8 == 0 and (s or n or layer):
                        pe.wait_ge(ct_ready, G * 2 + s // 8)
                    for u in range(GH):
                        last = mm(ps[32 * u:32 * u + 32, 6, :], vst[par][:, s % 8, u, :], pbuf[:, s % 2, u, :],
                                  start=(s % 8 == 0), stop=(s % 8 == 7))
                    last.then_inc(pv_done, 1)

                for s in range(16 if n < GROUPS else 3):
                    if s in at:
                        turn(layer, at[s][0], par, G, before + at[s][1], n == -2 and at[s][1] == 0 and not layer)
                    if s == 0 and n > -2 and n < GROUPS:
                        pe.wait_ge(turn_taken, before)
                    if s == 4 and takes_max:
                        pe.wait_ge(turn_taken, before + [t for t, _ in turns(n)].index("k_late") + 1)
                    if s == 8 and takes_max:
                        pe.wait_ge(turn_taken, before + [t for t, _ in turns(n)].index("q_late") + 1)
                    if s == 8 and attends:
                        pe.wait_ge(turn_taken, before + [t for t, _ in turns(n)].index("qm_late") + 1)
                    order = ("s0", "m0", "s1", "m1", "m2", "s2", "m3", "s3")
                    for what in order:
                        if what[0] == "s" and attends:
                            score(s, int(what[1]))
                        if what[0] == "m" and takes_max:
                            top(s, int(what[1]))
                    if s == 0:
                        if n >= 1:
                            weigh(15, G - 1, (par + 1) % 2)
                    elif attends:
                        weigh(s - 1, G, par)

            def chain_parts(layer, c, par):
                n = layer * CHUNKS + c
                first = isinstance(c, int) and c == 0 and layer == 0

                def turn_cx():
                    pe.wait_ge(cbuf_ready, n + 1)
                    if not first:
                        pe.wait_ge(wt_ready, n)
                    turn4(5, cbuf).then_inc(cx_turned, 1)

                def project_out():
                    pe.wait_ge(cxt_ready, n + 1)
                    if not first:
                        pe.wait_ge(lm_ready, n)
                    for j in range(4):
                        last = mm(ps[:, 4, j * P:(j + 1) * P], cxt[:, j * P:(j + 1) * P], wo_sb[:, :], start=True,
                                  stop=True)
                    last.then_inc(wo_done, 1)

                def turn_zn2():
                    pe.wait_ge(zn2_ready, n + 1)
                    turn4(5, zn2).then_inc(zn2_turned, 1)

                def logits():
                    pe.wait_ge(mt_ready, n + 1)
                    for j in range(4):
                        last = mm(ps[:, 4, j * EXPERTS:(j + 1) * EXPERTS], mt[par][:, j * P:(j + 1) * P],
                                  wg_sb[:, :], start=True, stop=True)
                    last.then_inc(logits_done, 1)

                def turn_w():
                    pe.wait_ge(w_ready, n + 1)
                    pe.transpose(ps[0:32, 5, 0:P], gate[:, 7, :], ident).then_inc(w_turned, 1)
                return turn_cx, project_out, turn_zn2, logits, turn_w

            def turn_out(layer, c):
                n = layer * CHUNKS + c
                pe.wait_ge(tmp_added, n * 7 + 7)
                if not (isinstance(c, int) and c == 0 and layer == 0):
                    pe.wait_ge(x_final, n)
                turn4(7, acc).then_inc(out_turned, 1)

            def experts(layer, c, par, at):
                n = layer * CHUNKS + c
                first = isinstance(c, int) and c == 0 and layer == 0

                def down(k):
                    e, f = k // FB, k % FB
                    pe.wait_ge(gelu_done, n * 32 + (k + 1))
                    if f == 0 and not (first and e < 2):
                        pe.wait_ge(tmp_ready, n * 8 + (e - 1))
                    last = mm(ps[:, 2 + e % 2, :], w2_sb[:, e, f, :], h1[k % 4], start=(f == 0), stop=(f == FB - 1))
                    if f == FB - 1:
                        last.then_inc(y_filled, 1)
                for k in range(32):
                    for f in at.get(k, ()):
                        f()
                    if not (first and k < 2):
                        pe.wait_ge(gelu_done, n * 32 + (k - 1))
                    mm(ps[:, k % 2, :], w1_sb[:, k // FB, k % FB * P:(k % FB + 1) * P], mt[par], start=True,
                       stop=True).then_inc(h_filled, 1)
                    if k >= 2:
                        down(k - 2)
                down(30)
                down(31)

            def mix(layer):
                for f in chain_parts(layer, 0, 0):
                    f()

                def one(c, par, before):
                    parts = chain_parts(layer, c + 1, (par + 1) % 2)
                    at = {1: (parts[0],), 3: (parts[1],), 10: (parts[2],), 13: (parts[3],), 19: (parts[4],)}
                    if before:
                        at[7] = (lambda: turn_out(layer, c - 1),)
                    experts(layer, c, par, at)
                one(0, 0, False)
                with pe.Fori(0, 3) as i:
                    one(i * 2 + 1, 1, True)
                    one(i * 2 + 2, 0, True)
                experts(layer, 7, 1, {7: (lambda: turn_out(layer, 6),)})
                turn_out(layer, 7)

            def retain():
                pe.wait_ge(x_final, CHUNKS)
                def one(c, first):
                    pe.wait_ge(rz_ready, c + 1)
                    if not first:
                        pe.wait_ge(rzt_ready, c)
                    turn4(7, zn[0]).then_inc(rz_turned, 1)
                    pe.wait_ge(rzt_ready, c + 1)
                    if not first:
                        pe.wait_ge(rq_ready, c)
                        pe.wait_ge(rk_ready, c)
                        pe.wait_ge(rkd_ready, c)
                        pe.wait_ge(rv_ready, c)
                    mm(ps[:, 0, :], rw_sb[:, 0:D], rzt, start=True, stop=True).then_inc(rq_done, 1)
                    mm(ps[:, 1, :], rw_sb[:, D:2 * D], rzt, start=True, stop=True).then_inc(rk_done, 1)
                    for b in range(BATCH):
                        last = mm(ps[:, 2 + b // 2, b % 2 * 256:b % 2 * 256 + 256], rzt[:, b * P:(b + 1) * P],
                                  rw_sb[:, 2 * D:4 * D], start=True, stop=True)
                    last.then_inc(rkv_done, 1)
                    pe.wait_ge(rq_ready, c + 1)
                    pe.wait_ge(rk_ready, c + 1)
                    if not first:
                        pe.wait_ge(ram_ready, c)
                    for b in range(BATCH):
                        cut = slice(b * P, (b + 1) * P)
                        last = mm(ps[:, 4, cut], rk[:, cut], rq[:, cut], start=True, stop=True)
                    last.then_inc(ra_done, 1)
                    pe.wait_ge(rkd_ready, c + 1)
                    pe.wait_ge(rv_ready, c + 1)
                    if not first:
                        pe.wait_ge(state_ready, c)
                    for b in range(BATCH):
                        cut = slice(b * P, (b + 1) * P)
                        last = mm(ps[:, 6, cut], rkd[:, cut], rv[:, cut], start=True, stop=True)
                    last.then_inc(rst_done, 1)
                    pe.wait_ge(ram_ready, c + 1)
                    pe.wait_ge(rqd_ready, c + 1)
                    if not first:
                        pe.wait_ge(rx_done, c)
                    for b in range(BATCH):
                        cut = slice(b * P, (b + 1) * P)
                        mm(ps[:, 5, cut], ram[:, cut], rv[:, cut], start=True, stop=False)
                        last = mm(ps[:, 5, cut], rqd[:, cut], state[:, cut], start=False, stop=True)
                    last.then_inc(ro_done, 1)
                one(0, True)
                with pe.Fori(1, KT) as c:
                    one(c, False)

            pe.wait_ge(w_loaded, 16 * W_DMAS)
            pe.wait_ge(consts_done, 1)
            for layer in range(2):
                project(layer)
                pe.wait_ge(qkv_stored, (layer + 1) * TILES)
                bodies(pe, lambda g, par, n: body(layer, g, par, n))
                mix(layer)
                if layer == 0:
                    retain()


def constants():
    import numpy as np
    i = np.arange(P, dtype=np.float64)
    t = np.zeros((P, C_END), np.float32)
    t[:, C_IDENT:C_IDENT + P] = np.eye(P)
    diff = i[None, :] - i[:, None]
    t[:, C_MASK:C_MASK + P] = np.where(diff >= 0, GAMMA ** np.maximum(diff, 0), 0.0)
    t[:, C_ROW:C_ROW + P] = GAMMA ** (i + 1)[None, :]
    t[:, C_COL] = GAMMA ** (P - 1 - i)
    t[:, C_RANK:C_RANK + EXPERTS] = EXPERTS - np.arange(EXPERTS)
    return t


def laid_out(L0_attn_x, L0_attn_weight_q, L0_attn_weight_k, L0_attn_weight_v, L0_attn_theta, L0_ffn_ln1_g,
             L0_ffn_ln1_b, L0_ffn_ln2_g, L0_ffn_ln2_b, L0_ffn_Wq, L0_ffn_Wk, L0_ffn_Wv, L0_ffn_Wo, L0_ffn_Wg,
             L0_ffn_W1, L0_ffn_b1, L0_ffn_W2, L0_ffn_b2):
    import numpy as np
    vectors = (L0_ffn_ln1_g, L0_ffn_ln1_b, L0_ffn_ln2_g, L0_ffn_ln2_b, L0_attn_theta)
    room = np.zeros((D, 3), np.float32)
    small = {"table": constants(), "cols": np.concatenate([np.stack(vectors, 1), room], 1),
             "wqkv": np.concatenate([L0_ffn_Wq, L0_ffn_Wk, L0_ffn_Wv], 1), "wo": L0_ffn_Wo, "wg": L0_ffn_Wg,
             "rw": np.concatenate([L0_attn_weight_q, L0_attn_weight_k, L0_attn_weight_v, L0_attn_weight_k], 1),
             "b1": L0_ffn_b1.reshape(EXPERTS * FB, P).T, "b2": L0_ffn_b2.T}
    return {"x": L0_attn_x.reshape(TILES, P, D).transpose(1, 0, 2).reshape(P, TILES * D),
            "small": np.concatenate([small[name] for name, _ in SMALL], 1),
            "w1": L0_ffn_W1.transpose(1, 0, 2),
            "w2": L0_ffn_W2.reshape(EXPERTS, FB, P, D).transpose(2, 0, 1, 3)}


def kernel(**inputs):
    import numpy as np
    import concourse.bacc as bacc
    from concourse.bass_utils import run_bass_kernel_spmd

    nc = bacc.Bacc("TRN2", target_bir_lowering=False, num_devices=1)
    arrays = laid_out(**{name: np.asarray(a) for name, a in inputs.items()})
    arrays = {name: np.ascontiguousarray(a) for name, a in arrays.items()}
    args = [nc.dram_tensor(f"in_{name}", a.shape, mybir.dt.from_np(a.dtype), kind="ExternalInput").ap()
            for name, a in arrays.items()]
    out = nc.dram_tensor("result", (P, TILES * D), F32, kind="ExternalOutput").ap()
    macaron(nc, *args, out)
    r = run_bass_kernel_spmd(nc, [{f"in_{name}": a for name, a in arrays.items()}], core_ids=[0])
    return r.results[0]["result"].reshape(P, TILES, D).transpose(1, 0, 2).reshape(BATCH, SEQ, D)
```

```python
from contextlib import ExitStack

import concourse.bass as bass
from concourse import mybir

ALU = mybir.AluOpType
ACT = mybir.ActivationFunctionType
F32 = mybir.dt.float32
F32R = mybir.dt.float32r
BF16 = mybir.dt.bfloat16
AX = mybir.AxisListType

P = 128
D = 128
BATCH, SEQ = 4, 1024
TOK = BATCH * SEQ
TILES = TOK // P
CHUNKS = TILES // 4
HEADS, DH = 16, 8
GH = 4
GROUPS = BATCH * HEADS // GH
KT = SEQ // P
ROWS = 64
EXPERTS, FF = 8, 512
FB = FF // P
EPS = 1e-5
SCALE = float(DH) ** -0.5
GAMMA = 0.96875
Q_PARTS = (0, 0, 1, 1, 0, 2)
K_PARTS = (0, 1, 0, 1, 2, 0)
MAX_ROW = 8 * len(Q_PARTS)
C_IDENT, C_MASK, C_ROW, C_COL, C_RANK, C_END = 0, 128, 256, 384, 385, 393

SMALL = (("table", C_END), ("cols", 8), ("wqkv", 3 * D), ("wo", D), ("wg", EXPERTS), ("rw", 4 * D),
         ("b1", EXPERTS * FB), ("b2", EXPERTS))

TURNS = (("k_late", 0), ("ctx1", 2), ("q_late", 3), ("qm_late", 6), ("ctx0", 10), ("qm_early", 11),
         ("k_early", 12), ("q_early", 14))


def turns(g):
    there = {"k_late": 0 <= g + 1 < GROUPS, "ctx1": 0 <= g - 1, "q_late": 0 <= g + 1 < GROUPS,
             "qm_late": 0 <= g < GROUPS, "ctx0": 0 <= g < GROUPS, "qm_early": 0 <= g + 1 < GROUPS,
             "k_early": 0 <= g + 2 < GROUPS, "q_early": 0 <= g + 2 < GROUPS}
    return [(name, s) for name, s in TURNS if there[name]]


def takes(name):
    return 2 if name in ("k_early", "k_late") else 1


def takes_in(g):
    return sum(takes(name) for name, _ in turns(g))


BODIES = list(range(-2, GROUPS + 1))
TAKES_OF_LAYER = sum(takes_in(g) for g in BODIES)
TURNS_OF_LAYER = sum(len(turns(g)) for g in BODIES)
FULL = len(TURNS)
LOOPED = (1, 13)


def turns_before(g):
    if isinstance(g, int):
        return sum(len(turns(i)) for i in BODIES if i < g)
    return g * FULL + (turns_before(1) - FULL)


def takes_before(g):
    if isinstance(g, int):
        return sum(takes_in(i) for i in BODIES if i < g)
    return g * takes_in(1) + (takes_before(1) - takes_in(1))


def takes_upto(g, name):
    names = [other for other, _ in turns(g)]
    return sum(takes(other) for other in names[:names.index(name) + 1])


def bodies(eng, emit):
    for g in (-2, -1, 0):
        emit(g, g % 2, g)
    with eng.Fori(0, (LOOPED[1] - LOOPED[0]) // 2) as i:
        emit(i * 2 + 1, 1, 1)
        emit(i * 2 + 2, 0, 2)
    for g in range(LOOPED[1], GROUPS + 1):
        emit(g, g % 2, g)


class Chain:

    def __init__(self, eng, sem, apart=None):
        self.eng, self.sem, self.n, self.base, self.apart = eng, sem, 0, 0, apart

    def link(self, ins):
        self.mark(ins)
        self.need()

    def mark(self, ins):
        self.n += 1
        ins.then_inc(self.sem, 1)

    def need(self):
        self.eng.wait_ge(self.sem, self.base + self.n)
        if self.apart and not isinstance(self.base, int):
            self.apart()

    def loop(self, i, per):
        self.start = self.n
        self.base = i * per

    def end(self, times, per):
        assert self.n == self.start + per, (self.n - self.start, per)
        self.n = self.start + times * per
        self.base = 0


def macaron(nc, x_in, small_in, w1, w2, out):
    with ExitStack() as ctx:
        def sb(name, shape, dt=F32):
            return ctx.enter_context(nc.sbuf_tensor(name, shape, dt))

        def sem(name):
            return ctx.enter_context(nc.semaphore(name))

        x = sb("x", [P, TILES * D])
        qkv = sb("qkv", [P, 3 * TILES * D])
        cx = qkv[:, 0:TILES * D]
        w1p = [sb(f"w1p{i}", [P, EXPERTS * FF], F32R) for i in range(2)]
        w2p = [sb(f"w2p{i}", [P, EXPERTS * FB * D], F32R) for i in range(2)]
        small = sb("small", [P, sum(w for _, w in SMALL)])
        at = dict(zip([name for name, _ in SMALL], [sum(w for _, w in SMALL[:i]) for i in range(len(SMALL))]))
        part = {name: small[:, at[name]:at[name] + w] for name, w in SMALL}
        wqkv_sb, wo_sb, wg_sb, rw_sb, b2_sb, tab = (part[n] for n in ("wqkv", "wo", "wg", "rw", "b2", "table"))
        b1_sb = part["b1"].rearrange("p (e f) -> p e f", e=EXPERTS)
        cols = part["cols"]
        ident_b = sb("ident_b", [P, P], BF16)
        st = sb("st", [P, TILES * 6])
        mean = sb("mean", [P, TILES])
        var = sb("var", [P, TILES])
        rstd = sb("rstd", [P, TILES])
        rstd2 = sb("rstd2", [P, TILES])
        shift = sb("shift", [P, TILES])
        sd = sb("sd", [P, TILES])
        ta = sb("ta", [P, TILES])
        tb = sb("tb", [P, TILES])
        gate = sb("gate", [P, 8, 32])
        gs = sb("gs", [P, 8, 4])
        st2 = sb("st2", [P, 4, 6])
        mv2 = sb("mv2", [P, 4, 2])
        ln2c = sb("ln2c", [P, 4, 4])
        wts_t = sb("wts_t", [32, P])[:, :]
        state = sb("state", [P, BATCH * D])
        with ExitStack() as phase:
            def at_(name, shape, dt=F32):
                return phase.enter_context(nc.sbuf_tensor(name, shape, dt))

            pbuf = at_("pbuf", [P, 2, GH, 512])
            q0 = [at_(f"q0{i}", [P, 2, 512], BF16) for i in range(2)]
            qm = [at_(f"qm{i}", [P, 2, 512], BF16) for i in range(2)]
            ct = at_("ct", [P, 512])
            rest = at_("rest", [P, 2, KT * GH * DH])
            nmax = at_("nmax", [P, 2, 2, 16])
            negm = at_("negm", [P, 16])
            negr = at_("negr", [P, 16])
            rden = at_("rden", [P, 16])
            kst = at_("kst", [P, KT, GH, ROWS], BF16)
            qst = [at_(f"qst{i}", [P, KT, GH, ROWS], BF16) for i in range(2)]
            vst = [at_(f"vst{i}", [P, KT, GH, 32]) for i in range(2)]
            kpad = [at_(f"kpad{i}", [P, GH, SEQ], BF16) for i in range(2)]
        with ExitStack() as phase:
            def at_(name, shape, dt=F32):
                return phase.enter_context(nc.sbuf_tensor(name, shape, dt))[:, :]

            cbuf, cxt, x2, zn2, mtf, acc = (at_(n, [P, 512]) for n in ("cbuf", "cxt", "x2", "zn2", "mtf", "acc"))
            tmp = [at_(f"tmp{i}", [P, 512]) for i in range(2)]
            hr = [at_(f"hr{i}", [P, 512]) for i in range(4)]
            hp = [[at_(f"hp{part}{i}", [P, 512], F32R) for i in range(4)] for part in range(2)]
            mtp = [[at_(f"mtp{part}{i}", [P, 512], F32R) for i in range(2)] for part in range(2)]
        with ExitStack() as phase:
            def at_(name, shape, dt=F32):
                return phase.enter_context(nc.sbuf_tensor(name, shape, dt))[:, :]

            zn = [at_(f"zn{i}", [P, 512]) for i in range(2)]
            ht = [at_(f"ht{i}", [P, 512]) for i in range(2)]
            rzt, rq, rk, rqd, rv, rkd = ([at_(f"{n}{i}", [P, 512]) for i in range(2)]
                                         for n in ("rzt", "rq", "rk", "rqd", "rv", "rkd"))
            ram = at_("ram", [P, 512])
        wbc = [qkv[:, 4096 * (i + 1):4096 * (i + 2)] for i in range(2)]
        w_dram = nc.dram_tensor("w_scratch", [2, 32, P], F32, kind="Internal").ap()

        ps = ctx.enter_context(nc.psum_tensor("ps", [P, 8, 512], F32))

        ident = tab[:, C_IDENT:C_IDENT + P]
        qkv5 = qkv[:, :].rearrange("p (a h n) -> p a h n", a=3, h=4)

        x_loaded, small_loaded, w_loaded, w_split = (sem("x_loaded"), sem("small_loaded"), sem("w_loaded"),
                                                     sem("w_split"))
        consts_done, theta_z, theta_e = sem("consts_done"), sem("theta_z"), sem("theta_e")
        stats_done, var_ready, sd_ready, norm_ready = (sem("stats_done"), sem("var_ready"),
                                                       sem("sd_ready"), sem("norm_ready"))
        dve_seq, pool_seq = sem("dve_seq"), sem("pool_seq")
        zn_ready, zn_turned, ht_ready, qkv_done, qkv_stored = (
            sem("zn_ready"), sem("zn_turned"), sem("ht_ready"), sem("qkv_done"), sem("qkv_stored"))
        kst_ready, qst_ready, vst_ready = sem("kst_ready"), sem("qst_ready"), sem("vst_ready")
        turned, turn_taken = sem("turned"), sem("turn_taken")
        max_filled, max_taken = sem("max_filled"), sem("max_taken")
        neg_ready = sem("neg_ready")
        s_filled, exp_done, pv_done, ct_ready = sem("s_filled"), sem("exp_done"), sem("pv_done"), sem("ct_ready")
        cbuf_ready, cx_turned, cxt_ready, wo_done, x2_ready, var2_ready, sd2_ready, norm2_ready = (
            sem("cbuf_ready"), sem("cx_turned"), sem("cxt_ready"), sem("wo_done"), sem("x2_ready"),
            sem("var2_ready"), sem("sd2_ready"), sem("norm2_ready"))
        zn2_ready, zn2_turned, mt_ready, logits_done, lm_ready, ex_ready, w_ready, w_turned, wt_ready = (
            sem("zn2_ready"), sem("zn2_turned"), sem("mt_ready"), sem("logits_done"), sem("lm_ready"),
            sem("ex_ready"), sem("w_ready"), sem("w_turned"), sem("wt_ready"))
        w_written, w_spread = sem("w_written"), sem("w_spread")
        mtf_ready, down_done, hh_ready, hl_even, hl_odd = (sem("mtf_ready"), sem("down_done"), sem("hh_ready"),
                                                           sem("hl_even"), sem("hl_odd"))
        h_filled, gelu_done, tmp_ready, tmp_added, out_turned, x_final = (
            sem("h_filled"), sem("gelu_done"), sem("tmp_ready"), sem("tmp_added"), sem("out_turned"),
            sem("x_final"))
        rz_ready, rz_turned, rzt_ready, rq_done, rk_done, rkv_done, rq_ready, rk_ready = (
            sem("rz_ready"), sem("rz_turned"), sem("rzt_ready"), sem("rq_done"), sem("rk_done"),
            sem("rkv_done"), sem("rq_ready"), sem("rk_ready"))
        rkd_ready, rv_ready, rqd_ready, ra_done, ram_ready, ro_done, rst_done, rx_done, state_ready = (
            sem("rkd_ready"), sem("rv_ready"), sem("rqd_ready"), sem("ra_done"), sem("ram_ready"),
            sem("ro_done"), sem("rst_done"), sem("rx_done"), sem("state_ready"))
        stored = sem("stored")

        block = ctx.enter_context(nc.Block())

        @block.sync
        def _(sp):
            for i in range(4):
                cut = slice(i * 1024, (i + 1) * 1024)
                sp.dma_start(x[:, cut], x_in[:, cut]).then_inc(x_loaded, 16)
            sp.dma_start(small[:, :], small_in).then_inc(small_loaded, 16)
            sp.dma_start(qkv[:, 0:4096], w1.rearrange("p e f -> p (e f)")).then_inc(w_loaded, 16)
            sp.dma_start(qkv[:, 4096:8192], w2.rearrange("p e f d -> p (e f d)")).then_inc(w_loaded, 16)

            def spread(layer, c, par):
                n = layer * CHUNKS + c
                sp.wait_ge(wt_ready, n + 1)
                sp.dma_start(w_dram[par], wts_t).then_inc(w_written, 16)
                sp.wait_ge(w_written, n * 16 + 16)
                if not (isinstance(c, int) and layer == 0 and c < 2):
                    sp.wait_ge(tmp_ready, n * 8 - 8)
                sp.dma_start(wbc[par], w_dram[par].rearrange("r t -> (r t)").partition_broadcast(P)
                             ).then_inc(w_spread, 16)

            def store(c):
                sp.wait_ge(x_final, CHUNKS + c + 1)
                cut = bass.ds(c * 512, 512)
                sp.dma_start(out[:, cut], x[:, cut]).then_inc(stored, 16)

            for layer in range(2):
                spread(layer, 0, 0)
                spread(layer, 1, 1)
                with sp.Fori(1, 4) as i:
                    for u in range(2):
                        if layer == 1:
                            store(i * 2 + (u - 2))
                        spread(layer, i * 2 + u, u)
            store(6)
            store(7)
            sp.wait_ge(stored, 16 * CHUNKS)

        @block.gpsimd
        def _(pool):
            def apart():
                pool.nop(nofuse=True)

            chain = Chain(pool, pool_seq, apart)
            def constant_parts():
                for i in range(2):
                    pool.memset(kpad[i][:, :, :].bitcast(F32), 0.0)
                    pool.memset(vst[i][:, :, :, :], 0.0)
                    pool.memset(qst[i][:, :, :, :].bitcast(F32), 0.0)
                chain.link(pool.memset(kst[:, :, :, :].bitcast(F32), 0.0))
                pool.memset(kst[:, :, :, MAX_ROW:MAX_ROW + 3], 1.0)
                for i in range(2):
                    last = pool.memset(vst[i][:, :, :, DH:DH + 1], 1.0)
                chain.link(last)

            def group_view(a, g):
                return qkv[:, bass.ds(g * 256 + a * TILES * D, 256)].rearrange(
                    "p (t h d) -> p t h d", t=KT, h=GH)

            def parts(a, g, dst, order):
                src = group_view(a, g)
                r = [rest[:, i, :].rearrange("p (t h d) -> p t h d", t=KT, h=GH) for i in range(2)]

                def rows(j):
                    return dst[:, :, :, 8 * j:8 * j + 8]

                level = [[j for j, part in enumerate(order) if part == n] for n in range(3)]
                for j in level[0][1:]:
                    pool.tensor_copy(rows(j), src)
                chain.link(pool.tensor_copy(rows(level[0][0]), src))
                chain.link(pool.tensor_tensor(r[0], src, rows(level[0][0]), ALU.subtract))
                for j in level[1][1:]:
                    pool.tensor_copy(rows(j), r[0])
                chain.link(pool.tensor_copy(rows(level[1][0]), r[0]))
                chain.link(pool.tensor_tensor(r[1], r[0], rows(level[1][0]), ALU.subtract))
                return pool.tensor_copy(rows(level[2][0]), r[1])

            def body(layer, g, par, n):
                at = dict((name, i) for i, (name, _) in enumerate(turns(n)))
                before = turns_before(g) + layer * TURNS_OF_LAYER
                G = g + layer * GROUPS
                if 0 <= n + 1 < GROUPS:
                    if n >= 1 or layer:
                        pool.wait_ge(ct_ready, G * 2)
                        apart()
                    pool.tensor_copy(vst[(par + 1) % 2][:, :, :, 0:DH],
                                     group_view(2, g + 1)).then_inc(vst_ready, 1)
                if 0 <= n + 2 < GROUPS:
                    if n >= -1:
                        pool.wait_ge(turned, before + at["k_late"] + 1)
                        apart()
                    parts(1, g + 2, kst, K_PARTS).then_inc(kst_ready, 1)
                    if n >= 0:
                        pool.wait_ge(turned, before + at["qm_late"] + 1)
                        apart()
                    chain.link(pool.memset(qst[par][:, :, :, MAX_ROW:MAX_ROW + 3], 0.0))
                    parts(0, g + 2, qst[par], Q_PARTS).then_inc(qst_ready, 1)

            def attend(layer):
                constant_parts()
                pool.wait_ge(qkv_stored, (layer + 1) * TILES)
                body(layer, -2, 0, -2)
                body(layer, -1, 1, -1)
                body(layer, 0, 0, 0)
                with pool.Fori(0, 6) as i:
                    chain.loop(i, 18)
                    body(layer, i * 2 + 1, 1, 1)
                    body(layer, i * 2 + 2, 0, 2)
                    chain.end(6, 18)
                for g in range(13, GROUPS + 1):
                    body(layer, g, g % 2, g)

            def gather_cx(layer, c):
                n = layer * CHUNKS + c
                if not isinstance(c, int) or c or layer:
                    pool.wait_ge(cx_turned, n)
                    apart()
                pool.tensor_copy(cbuf.rearrange("p (t h n) -> p h t n", t=4, h=4),
                                 cx.rearrange("p (h n) -> p h n", h=4)[:, :, bass.ds(c * 128, 128)]
                                 .rearrange("p h (t n) -> p h t n", t=4)).then_inc(cbuf_ready, 1)

            def sum_experts(layer, c):
                n = layer * CHUNKS + c
                first = isinstance(c, int) and c == 0 and layer == 0
                for k in range(1, 32, 2):
                    if k == 5 and not (isinstance(c, int) and c == 0):
                        add_expert(n - 1, EXPERTS - 1, False)
                    pool.wait_ge(hh_ready, n * 32 + (k + 1))
                    pool.tensor_tensor(hp[1][k % 4], hr[k % 4], hp[0][k % 4].bitcast(F32),
                                       ALU.subtract).then_inc(hl_odd, 1)
                    e = (k - 7) // 4
                    if k % 4 != 3 or e < 1:
                        continue
                    add_expert(n, e, first)

            def add_expert(n, e, first):
                pool.wait_ge(tmp_ready, n * 8 + (e + 1))
                if e == 1:
                    if not first:
                        pool.wait_ge(out_turned, n)
                    ins = pool.tensor_tensor(acc, tmp[0], tmp[1], ALU.add)
                else:
                    pool.wait_ge(tmp_added, n * 7 + (e - 1))
                    ins = pool.tensor_tensor(acc, acc, tmp[e % 2], ALU.add)
                ins.then_inc(tmp_added, 1)

            def mix(layer):
                pool.wait_ge(turn_taken, (layer + 1) * TAKES_OF_LAYER)
                gather_cx(layer, 0)
                gather_cx(layer, 1)
                sum_experts(layer, 0)
                with pool.Fori(1, 7) as c:
                    gather_cx(layer, c + 1)
                    sum_experts(layer, c)
                sum_experts(layer, CHUNKS - 1)
                add_expert((layer + 1) * CHUNKS - 1, EXPERTS - 1, False)

            def retain():
                def one(c, u):
                    pool.wait_ge(rq_ready, c + 1)
                    pool.tensor_tensor(rqd[u].rearrange("p (b t) -> p b t", b=BATCH),
                                       rq[u].rearrange("p (b t) -> p b t", b=BATCH),
                                       tab[:, C_ROW:C_ROW + P].unsqueeze(1).broadcast_to([P, BATCH, P]),
                                       ALU.mult).then_inc(rqd_ready, 1)
                with pool.Fori(0, KT // 2) as i:
                    one(i * 2, 0)
                    one(i * 2 + 1, 1)
                pool.wait_ge(rx_done, KT)

            pool.memset(state[:, :], 0.0)
            pool.wait_ge(small_loaded, 16)
            for layer in range(2):
                attend(layer)
                mix(layer)
                if layer == 0:
                    retain()

        @block.scalar
        def _(act):
            def std(n):
                act.wait_ge(var_ready, n)
                act.activation(sd[:, :], ta[:, :], ACT.Sqrt).then_inc(sd_ready, 1)

            def normed(dst, c, n):
                if not isinstance(c, int) or n > 1:
                    act.wait_ge(zn_turned, n - 1)
                for j in range(4):
                    t = c * 4 + j
                    last = act.activation(dst[:, j * D:(j + 1) * D], x[:, bass.ds(t * D, D)], ACT.Identity,
                                          scale=rstd2[:, bass.ds(t, 1)], bias=shift[:, bass.ds(t, 1)])
                last.then_inc(zn_ready, 1)

            def keep_qkv(layer, c):
                if layer == 0 and isinstance(c, int) and c == 0:
                    act.wait_ge(w_split, 4)
                for j in range(4):
                    t = c * 4 + j
                    act.wait_ge(qkv_done, layer * TILES + t + 1)
                    act.activation(qkv5[:, :, :, bass.ds(t * 32, 32)],
                                   ps[:, j, 0:3 * D].rearrange("p (a h n) -> p a h n", a=3, h=4),
                                   ACT.Copy).then_inc(qkv_stored, 1)

            def split_weights():
                act.wait_ge(w_loaded, 32)
                for i, halves in enumerate((w1p, w2p)):
                    act.activation(halves[0][:, :], qkv[:, i * 4096:(i + 1) * 4096],
                                   ACT.Copy).then_inc(w_split, 1)

            def project(layer):
                n = layer * CHUNKS
                std(3 * layer + 1)
                std(3 * layer + 2)
                act.wait_ge(norm_ready, 2 * layer + 1)
                normed(zn[0], 0, n)
                normed(zn[1], 1, n + 1)
                if layer == 0:
                    split_weights()
                keep_qkv(layer, 0)
                normed(zn[0], 2, n + 2)
                keep_qkv(layer, 1)
                normed(zn[1], 3, n + 3)
                with act.Fori(1, 3) as i:
                    for u in range(2):
                        keep_qkv(layer, i * 2 + u)
                        normed(zn[u], i * 2 + (u + 2), i * 2 + (n + u + 2))
                keep_qkv(layer, 6)
                keep_qkv(layer, 7)

            def take_turn(name, par, count):
                act.wait_ge(turned, count)
                src = ps[:, 7, :].bitcast(BF16).rearrange("p (a n) -> p a n", a=2)
                if name in ("k_early", "k_late"):
                    kh = 512 * (name == "k_late")
                    k2 = (par + (name == "k_late")) % 2
                    last = act.activation(kpad[k2][0:64, 0:GH:2, kh:kh + 512], src[0:64, :, :], ACT.Copy)
                else:
                    dst = {"q_early": q0[0], "q_late": q0[1], "qm_early": qm[0], "qm_late": qm[1]}[name]
                    last = act.activation(dst[:, :, :], src, ACT.Copy)
                last.then_inc(turn_taken, 1)

            def body(layer, g, par, n):
                G = g + layer * GROUPS
                at = {s: (name, i) for i, (name, s) in enumerate(turns(n))}
                before = turns_before(g) + layer * TURNS_OF_LAYER

                def between(s):
                    if (s == 1 and n >= 1) or (s == 9 and 0 <= n < GROUPS):
                        act.wait_ge(pv_done, G * 16 + (s - 1))
                        act.activation(ct[:, :], ps[:, 6, :], ACT.Copy).then_inc(ct_ready, 1)
                    if s in at and not at[s][0].startswith("ctx"):
                        take_turn(at[s][0], par, before + (at[s][1] + 1))

                for s in range(16 if n < GROUPS else 3):
                    if 0 <= n < GROUPS:
                        for u in range(GH):
                            if u == 2:
                                between(s)
                            act.wait_ge(s_filled, G * 64 + (4 * s + u + 1))
                            if u == 0 and (n > 0 or s > 1 or layer):
                                act.wait_ge(pv_done, G * 16 + (s - 1))
                            act.activation(pbuf[:, s % 2, u, :], ps[:, u % 2, :], ACT.Exp,
                                           scale=SCALE).then_inc(exp_done, 1)
                    else:
                        between(s)

            def gelus(layer, c, after):
                n = layer * CHUNKS + c
                for k in range(32):
                    act.wait_ge(h_filled, n * 32 + (k + 1))
                    if k >= 4 or not (isinstance(c, int) and c == 0 and layer == 0):
                        act.wait_ge(hh_ready, n * 32 + (k - 3))
                        act.wait_ge(hl_odd if k % 2 else hl_even, n * 16 + (k // 2 - 1))
                    act.activation(hr[k % 4], ps[:, k % 4, :], ACT.Gelu_apprx_tanh,
                                   bias=b1_sb[:, k // 4, k % 4:k % 4 + 1]).then_inc(gelu_done, 1)
                    for f in after.get(k, ()):
                        f()

            def chain_parts(layer, c, par):
                n = layer * CHUNKS + c

                def copy_cx():
                    act.wait_ge(cx_turned, n + 1)
                    act.activation(cxt, ps[:, 7, :], ACT.Copy).then_inc(cxt_ready, 1)

                def root():
                    act.wait_ge(var2_ready, n + 1)
                    act.activation(ln2c[:, 1, :], ln2c[:, 0, :], ACT.Sqrt).then_inc(sd2_ready, 1)

                def norm():
                    act.wait_ge(norm2_ready, n + 1)
                    for j in range(4):
                        last = act.activation(zn2[:, j * D:(j + 1) * D], x2[:, j * D:(j + 1) * D], ACT.Identity,
                                              scale=ln2c[:, 2, j:j + 1], bias=ln2c[:, 3, j:j + 1])
                    last.then_inc(zn2_ready, 1)

                def affine():
                    act.wait_ge(zn2_turned, n + 1)
                    act.activation(mtf, ps[:, 7, :], ACT.Identity, scale=cols[:, 2:3],
                                   bias=cols[:, 3:4]).then_inc(mtf_ready, 1)

                def expo():
                    act.wait_ge(lm_ready, n + 1)
                    act.activation(gate[:, 1, :], gate[:, 0, :], ACT.Exp).then_inc(ex_ready, 1)
                return copy_cx, root, norm, affine, expo

            def mix(layer):
                for f in chain_parts(layer, 0, 0):
                    f()

                def one(c, par):
                    copy_cx, root, norm, affine, expo = chain_parts(layer, c + 1, (par + 1) % 2)
                    gelus(layer, c, {1: (copy_cx,), 6: (root,), 8: (norm,), 11: (affine,), 16: (expo,)})
                one(0, 0)
                with act.Fori(0, 3) as i:
                    one(i * 2 + 1, 1)
                    one(i * 2 + 2, 0)
                gelus(layer, 7, {})

            def retain():
                act.wait_ge(theta_z, 1)
                act.activation(cols[:, 6:7], cols[:, 5:6], ACT.Exp).then_inc(theta_e, 1)
                std(3)
                act.wait_ge(norm_ready, 2)
                act.wait_ge(theta_e, 2)

                def normed_x(c, u, first):
                    if not first:
                        act.wait_ge(rz_turned, c - 1)
                    for b in range(BATCH):
                        t = c + b * KT
                        last = act.activation(zn[u][:, b * D:(b + 1) * D], x[:, bass.ds(t * D, D)], ACT.Identity,
                                              scale=rstd[:, bass.ds(t, 1)], bias=shift[:, bass.ds(t, 1)])
                    last.then_inc(rz_ready, 1)

                def operands(c, u, first):
                    if not first:
                        act.wait_ge(ro_done, c - 1)
                    act.wait_ge(rq_done, c + 1)
                    act.activation(rq[u], ps[:, 0, :], ACT.Copy, scale=cols[:, 7:8]).then_inc(rq_ready, 1)
                    act.wait_ge(rk_done, c + 1)
                    act.activation(rk[u], ps[:, 1, :], ACT.Copy).then_inc(rk_ready, 1)
                    act.wait_ge(rkv_done, c + 1)
                    act.activation(rkd[u].rearrange("p (b d) -> p b d", b=BATCH),
                                   ps[:, 2:4, :].rearrange("p a (b n) -> p (a b) n", b=2)[:, :, D:2 * D],
                                   ACT.Copy, scale=tab[:, C_COL:C_COL + 1]).then_inc(rkd_ready, 1)
                normed_x(0, 0, True)
                normed_x(1, 1, True)
                operands(0, 0, True)
                normed_x(2, 0, False)
                operands(1, 1, True)
                normed_x(3, 1, False)
                with act.Fori(1, KT // 2 - 1) as i:
                    for u in range(2):
                        operands(i * 2 + u, u, False)
                        normed_x(i * 2 + (u + 2), u, False)
                operands(KT - 2, 0, False)
                operands(KT - 1, 1, False)

            act.wait_ge(small_loaded, 16)
            for layer in range(2):
                project(layer)
                bodies(act, lambda g, par, n: body(layer, g, par, n))
                mix(layer)
                if layer == 0:
                    retain()

        @block.vector
        def _(dve):
            chain = Chain(dve, dve_seq)

            def stats(n):
                with dve.Fori(0, CHUNKS) as i:
                    for j in range(4):
                        dve.bn_stats(st[:, bass.ds(i * 24 + j * 6, 6)],
                                     x[:, bass.ds(i * 512 + j * D, D)]).then_inc(stats_done, 1)
                dve.wait_ge(stats_done, TILES * (n + 1))
                s = st[:, :].rearrange("p (t c) -> p t c", c=6)
                dve.tensor_tensor(ta[:, :], s[:, :, 1], s[:, :, 4], ALU.subtract)
                dve.tensor_tensor(tb[:, :], s[:, :, 2], s[:, :, 5], ALU.add)
                chain.link(dve.tensor_tensor(mean[:, :], s[:, :, 1], s[:, :, 4], ALU.add))
                dve.tensor_scalar(mean[:, :], mean[:, :], 0.5, None, ALU.mult)
                dve.tensor_scalar(tb[:, :], tb[:, :], 1.0 / D, None, ALU.mult)
                chain.link(dve.tensor_tensor(ta[:, :], ta[:, :], ta[:, :], ALU.mult))
                chain.link(dve.scalar_tensor_tensor(out=var[:, :], in0=ta[:, :], scalar=0.25, in1=tb[:, :],
                                                    op0=ALU.mult, op1=ALU.add))
                dve.tensor_scalar(ta[:, :], var[:, :], EPS, None, ALU.add).then_inc(var_ready, 1)

            def ht_evac(c, u, n):
                dve.wait_ge(zn_turned, n + 1)
                dve.tensor_scalar(ht[u], ps[:, 6 + u, :], cols[:, 0:1], cols[:, 1:2], ALU.mult,
                                  ALU.add).then_inc(ht_ready, 1)

            def project(layer):
                if layer == 0:
                    dve.wait_ge(x_loaded, 64)
                stats(2 * layer)
                dve.wait_ge(sd_ready, 3 * layer + 1)
                chain.link(dve.reciprocal(rstd[:, :], sd[:, :]))
                chain.link(dve.tensor_tensor(tb[:, :], rstd[:, :], rstd[:, :], ALU.mult))
                chain.link(dve.tensor_tensor(tb[:, :], tb[:, :], var[:, :], ALU.mult))
                dve.tensor_scalar(ta[:, :], tb[:, :], EPS, None, ALU.add).then_inc(var_ready, 1)
                dve.wait_ge(sd_ready, 3 * layer + 2)
                chain.link(dve.reciprocal(rstd2[:, :], sd[:, :]))
                chain.link(dve.tensor_tensor(rstd2[:, :], rstd2[:, :], rstd[:, :], ALU.mult))
                dve.scalar_tensor_tensor(out=shift[:, :], in0=mean[:, :], scalar=-1.0, in1=rstd2[:, :],
                                         op0=ALU.mult, op1=ALU.mult).then_inc(norm_ready, 1)
                if layer == 0:
                    for i, halves in enumerate((w1p, w2p)):
                        dve.wait_ge(w_split, i + 2)
                        dve.tensor_tensor(halves[1][:, :], qkv[:, i * 4096:(i + 1) * 4096],
                                          halves[0][:, :].bitcast(F32), ALU.subtract).then_inc(w_split, 1)
                with dve.Fori(0, CHUNKS // 2) as i:
                    for u in range(2):
                        ht_evac(i * 2 + u, u, i * 2 + (layer * CHUNKS + u))

            def neg_step(layer, g, par, half, k):
                col = qst[par][:, 4 * half:4 * half + 4, :, :]
                a = negm[:, :].rearrange("p (t h) -> p t h", t=4)
                r = negr[:, :].rearrange("p (t h) -> p t h", t=4)
                part = [col[:, :, :, MAX_ROW + i] for i in range(3)]
                if k == 0:
                    link = dve.tensor_tensor(negm[:, :], nmax[:, half, 0, :], nmax[:, half, 1, :], ALU.min)
                elif k == 1:
                    link = dve.tensor_copy(part[0], a)
                elif k == 2:
                    link = dve.tensor_tensor(r, a, part[0], ALU.subtract)
                elif k == 3:
                    link = dve.tensor_copy(part[1], r)
                elif k == 4:
                    link = dve.tensor_tensor(a, r, part[1], ALU.subtract)
                else:
                    dve.tensor_copy(part[2], a).then_inc(neg_ready, 1)
                    return
                chain.mark(link)

            def body(layer, g, par, n):
                G = g + layer * GROUPS
                at = {s: (name, i) for i, (name, s) in enumerate(turns(n))}
                before = turns_before(g) + layer * TURNS_OF_LAYER
                steps = []

                def next_step():
                    if steps:
                        half, k = steps.pop(0)
                        if k == 0:
                            dve.wait_ge(max_taken, (G + 1) * 64 + (0 if half else 32))
                        else:
                            chain.need()
                        neg_step(layer, g if half else g + 1, par if half else (par + 1) % 2, half, k)

                for s in range(16 if n < GROUPS else 3):
                    half, kh, j = s // 8, s % 8 // 4, s % 4
                    if s == 0 and 0 <= n < GROUPS:
                        steps += [(1, k) for k in range(6)]
                    if s == 8 and 0 <= n + 1 < GROUPS:
                        steps += [(0, k) for k in range(6)]
                    for u in range(GH):
                        next_step()
                        if 0 <= n + 1 < GROUPS:
                            dve.wait_ge(max_filled, (G + 1) * 64 + (4 * s + u + 1))
                            dve.tensor_reduce(nmax[:, half, kh, 4 * j + u:4 * j + u + 1], ps[:, 2 + u, :],
                                              AX.X, ALU.max, negate=True).then_inc(max_taken, 1)
                        if u == 1 and s in at and at[s][0] in ("k_early", "k_late"):
                            name, i = at[s]
                            late = name == "k_late"
                            dve.wait_ge(turned, before + i + 1)
                            src = ps[:, 7, :].bitcast(BF16).rearrange("p (a n) -> p a n", a=2)
                            dve.tensor_copy(kpad[(par + late) % 2][64:128, 1:GH:2, 512 * late:512 * late + 512],
                                            src[64:128, :, :]).then_inc(turn_taken, 1)
                    if s in at and at[s][0].startswith("ctx"):
                        name, i = at[s]
                        half_done = 1 if name == "ctx1" else 0
                        dve.wait_ge(turned, before + i + 1)
                        src = ps[:, 7, :].rearrange("p (t h n) -> p t h n", t=4, h=GH)
                        rd = rden[:, :].rearrange("p (t h) -> p t h", t=4)
                        chain.link(dve.reciprocal(rd, src[:, :, :, DH]))
                        g2 = g if name == "ctx0" else g - 1
                        dve.tensor_tensor(
                            cx[:, bass.ds(g2 * 256 + half_done * 128, 128)].rearrange(
                                "p (t h n) -> p t h n", t=4, h=GH),
                            src[:, :, :, 0:DH], rd.unsqueeze(3).broadcast_to([P, 4, GH, DH]),
                            ALU.mult).then_inc(turn_taken, 1)

            def attend(layer):
                for g in (-2, -1, 0):
                    body(layer, g, g % 2, g)
                with dve.Fori(0, 6) as i:
                    chain.loop(i, 24)
                    body(layer, i * 2 + 1, 1, 1)
                    body(layer, i * 2 + 2, 0, 2)
                    chain.end(6, 24)
                for g in range(13, GROUPS + 1):
                    body(layer, g, g % 2, g)

            g3 = [gate[:, i, :].rearrange("p (t e) -> p t e", t=4) for i in range(8)]
            rank = tab[:, C_RANK:C_RANK + EXPERTS].unsqueeze(1).broadcast_to([P, 4, EXPERTS])

            def bc(i):
                return gs[:, i, :].unsqueeze(2).broadcast_to([P, 4, EXPERTS])

            def chain_parts(layer, c, par):
                n = layer * CHUNKS + c

                def residual():
                    if not (isinstance(c, int) and c == 0 and layer == 0):
                        dve.wait_ge(zn2_ready, n)
                    xs = x[:, bass.ds(c * 512, 512)]
                    for j in range(4):
                        t = c * 4 + j
                        last = dve.tensor_scalar(x2[:, j * D:(j + 1) * D], x[:, bass.ds(t * D, D)],
                                                 mean[:, bass.ds(t, 1)], rstd[:, bass.ds(t, 1)],
                                                 ALU.subtract, ALU.mult)
                    chain.link(last)
                    dve.wait_ge(wo_done, n + 1)
                    chain.link(dve.tensor_tensor(x2, ps[:, 6, :], x2, ALU.add))
                    for j in range(4):
                        last = dve.bn_stats(st2[:, j, :], x2[:, j * D:(j + 1) * D])
                    chain.link(last)
                    dve.nop(nofuse=True)
                    for j in range(4):
                        last = dve.bn_aggr(mv2[:, j, :], st2[:, j, :])
                    chain.link(last)
                    dve.tensor_scalar(ln2c[:, 0, :], mv2[:, :, 1], EPS, None, ALU.add).then_inc(var2_ready, 1)
                    dve.scalar_tensor_tensor(out=xs, in0=x2, scalar=0.5, in1=xs, op0=ALU.mult,
                                             op1=ALU.add).then_inc(x2_ready, 1)

                def shift2():
                    dve.wait_ge(sd2_ready, n + 1)
                    chain.link(dve.reciprocal(ln2c[:, 2, :], ln2c[:, 1, :]))
                    dve.scalar_tensor_tensor(out=ln2c[:, 3, :], in0=mv2[:, :, 0], scalar=-1.0, in1=ln2c[:, 2, :],
                                             op0=ALU.mult, op1=ALU.mult).then_inc(norm2_ready, 1)

                def split_m():
                    dve.wait_ge(mtf_ready, n + 1)
                    chain.link(dve.tensor_copy(mtp[0][par], mtf))
                    dve.tensor_tensor(mtp[1][par], mtf, mtp[0][par].bitcast(F32),
                                      ALU.subtract).then_inc(mt_ready, 1)

                def gate1():
                    dve.wait_ge(logits_done, n + 1)
                    lg = ps[:, 6, 0:32].rearrange("p (t e) -> p t e", t=4)
                    chain.link(dve.tensor_reduce(gs[:, 0, :], lg, AX.X, ALU.max))
                    dve.tensor_tensor(g3[0], lg, bc(0), ALU.subtract).then_inc(lm_ready, 1)

                def gate2():
                    dve.wait_ge(ex_ready, n + 1)
                    chain.link(dve.tensor_reduce(gs[:, 1, :], g3[1], AX.X, ALU.add))
                    chain.link(dve.reciprocal(gs[:, 1, :], gs[:, 1, :]))
                    chain.link(dve.tensor_tensor(g3[2], g3[1], bc(1), ALU.mult))

                    def top(src, value, onehot):
                        chain.link(dve.tensor_reduce(gs[:, value, :], src, AX.X, ALU.max))
                        chain.link(dve.tensor_tensor(g3[6], src, bc(value), ALU.is_equal))
                        chain.link(dve.tensor_tensor(g3[6], g3[6], rank, ALU.mult))
                        chain.link(dve.tensor_reduce(gs[:, 4, :], g3[6], AX.X, ALU.max))
                        chain.link(dve.tensor_tensor(g3[onehot], bc(4), rank, ALU.is_equal))
                    top(g3[2], 2, 3)
                    chain.link(dve.scalar_tensor_tensor(out=g3[4], in0=g3[3], scalar=-2.0, in1=g3[2],
                                                        op0=ALU.mult, op1=ALU.add))
                    top(g3[4], 3, 5)
                    dve.tensor_tensor(g3[3], g3[3], g3[5], ALU.add)
                    chain.link(dve.tensor_tensor(gs[:, 5, :], gs[:, 2, :], gs[:, 3, :], ALU.add))
                    chain.link(dve.reciprocal(gs[:, 5, :], gs[:, 5, :]))
                    chain.link(dve.tensor_tensor(g3[3], g3[3], g3[2], ALU.mult))
                    if not (isinstance(c, int) and c == 0 and layer == 0):
                        dve.wait_ge(w_turned, n)
                    dve.tensor_tensor(gate[:, 7, :].rearrange("p (e t) -> p t e", e=EXPERTS), g3[3], bc(5),
                                      ALU.mult).then_inc(w_ready, 1)

                def copy_w():
                    dve.wait_ge(w_turned, n + 1)
                    if not (isinstance(c, int) and c == 0 and layer == 0):
                        dve.wait_ge(w_written, n * 16)
                    dve.tensor_copy(wts_t, ps[0:32, 7, 0:128]).then_inc(wt_ready, 1)
                return residual, shift2, split_m, gate1, gate2, copy_w

            CHAIN_LINKS = 4 + 1 + 1 + 1 + (3 + 5 + 1 + 5 + 3)

            def expert(n, par, e, first):
                if e == 0:
                    dve.wait_ge(w_spread, n * 16 + 16)
                dve.wait_ge(down_done, n * 32 + (FB * e + FB))
                if e >= 2:
                    dve.wait_ge(tmp_added, n * 7 + max(e - 2, 1))
                elif not first:
                    dve.wait_ge(tmp_added, n * 7)
                dve.scalar_tensor_tensor(out=tmp[e % 2], in0=ps[:, 4 + e % 2, :], scalar=b2_sb[:, e:e + 1],
                                         in1=wbc[par][:, e * 512:(e + 1) * 512], op0=ALU.add,
                                         op1=ALU.mult).then_inc(tmp_ready, 1)

            def finish(layer, c):
                n = layer * CHUNKS + c
                dve.wait_ge(out_turned, n + 1)
                xs = x[:, bass.ds(c * 512, 512)]
                dve.scalar_tensor_tensor(out=xs, in0=ps[:, 7, :], scalar=0.5, in1=xs, op0=ALU.mult,
                                         op1=ALU.add).then_inc(x_final, 1)

            def mix(layer):
                for f in chain_parts(layer, 0, 0):
                    f()

                def one(c, par, before, after):
                    n = layer * CHUNKS + c
                    first = not before and layer == 0
                    parts = chain_parts(layer, c + 1, (par + 1) % 2) if after else None
                    at = dict(zip((4, 7, 12, 16, 19, 25), parts or ()))
                    for k in range(EXPERTS * FB):
                        dve.wait_ge(gelu_done, n * 32 + (k + 1))
                        if k >= 4 or not first:
                            dve.wait_ge(down_done, n * 32 + (k - 3))
                        dve.tensor_copy(hp[0][k % 4], hr[k % 4]).then_inc(hh_ready, 1)
                        if k % 2:
                            dve.wait_ge(hh_ready, n * 32 + k)
                            dve.tensor_tensor(hp[1][(k - 1) % 4], hr[(k - 1) % 4],
                                              hp[0][(k - 1) % 4].bitcast(F32), ALU.subtract).then_inc(hl_even, 1)
                        if k == 3 and before:
                            expert(n - 1, (par + 1) % 2, EXPERTS - 1, False)
                        if k % 4 == 3 and k >= 7:
                            expert(n, par, (k - 7) // 4, first)
                        if k == 9 and before:
                            finish(layer, c - 1)
                        if k in at:
                            at[k]()
                one(0, 0, False, True)
                with dve.Fori(0, 3) as i:
                    chain.loop(i, 2 * CHAIN_LINKS)
                    one(i * 2 + 1, 1, True, True)
                    one(i * 2 + 2, 0, True, True)
                    chain.end(3, 2 * CHAIN_LINKS)
                one(7, 1, True, False)
                expert((layer + 1) * CHUNKS - 1, 1, EXPERTS - 1, False)
                finish(layer, 7)

            def retain():
                chain.link(dve.tensor_scalar(cols[:, 5:6], cols[:, 4:5], 0.0, None, ALU.mult))
                dve.tensor_copy(cols[:, 5:6], cols[:, 5:6]).then_inc(theta_z, 1)
                dve.wait_ge(x_final, CHUNKS)
                stats(1)
                dve.wait_ge(sd_ready, 3)
                chain.link(dve.reciprocal(rstd[:, :], sd[:, :]))
                dve.scalar_tensor_tensor(out=shift[:, :], in0=mean[:, :], scalar=-1.0, in1=rstd[:, :],
                                         op0=ALU.mult, op1=ALU.mult).then_inc(norm_ready, 1)
                dve.wait_ge(theta_e, 1)
                dve.tensor_tensor(cols[:, 7:8], cols[:, 6:7], cols[:, 6:7], ALU.mult).then_inc(theta_e, 1)
                b4 = "p (b n) -> p b n"

                def turned_z(c, u):
                    dve.wait_ge(rz_turned, c + 1)
                    dve.tensor_copy(rzt[u], ps[:, 7, :]).then_inc(rzt_ready, 1)

                def values(c, u):
                    dve.wait_ge(rkd_ready, c + 1)
                    dve.tensor_copy(rv[u].rearrange(b4, b=BATCH),
                                    ps[:, 2:4, :].rearrange("p a (b n) -> p (a b) n", b=2)[:, :, 0:D]
                                    ).then_inc(rv_ready, 1)

                def step(c, u, last=False):
                    if not last:
                        turned_z(c + 1, 1 - u)
                    dve.wait_ge(ra_done, c + 1)
                    dve.tensor_tensor(ram.rearrange(b4, b=BATCH), ps[:, 4, :].rearrange(b4, b=BATCH),
                                      tab[:, C_MASK:C_MASK + P].unsqueeze(1).broadcast_to([P, BATCH, P]),
                                      ALU.mult).then_inc(ram_ready, 1)
                    if not last:
                        values(c + 1, 1 - u)
                    dve.wait_ge(ro_done, c + 1)
                    xs = x[:, :].rearrange(b4, b=BATCH)[:, :, bass.ds(c * D, D)]
                    dve.tensor_tensor(xs, ps[:, 5, :].rearrange(b4, b=BATCH), xs, ALU.add).then_inc(rx_done, 1)
                    dve.wait_ge(rst_done, c + 1)
                    dve.scalar_tensor_tensor(out=state[:, :], in0=state[:, :], scalar=GAMMA ** P,
                                             in1=ps[:, 6, :], op0=ALU.mult, op1=ALU.add
                                             ).then_inc(state_ready, 1)
                turned_z(0, 0)
                values(0, 0)
                step(0, 0)
                with dve.Fori(0, KT // 2 - 1) as i:
                    step(i * 2 + 1, 1)
                    step(i * 2 + 2, 0)
                step(KT - 1, 1, last=True)
                dve.wait_ge(rx_done, KT)

            dve.wait_ge(small_loaded, 16)
            dve.tensor_copy(ident_b[:, :], ident).then_inc(consts_done, 1)
            for layer in range(2):
                project(layer)
                attend(layer)
                mix(layer)
                if layer == 0:
                    retain()

        @block.tensor
        def _(pe):
            mm = pe.matmul

            def turn4(bank, src):
                for j in range(4):
                    last = pe.transpose(ps[:, bank, j * P:(j + 1) * P], src[:, j * P:(j + 1) * P], ident)
                return last

            def project(layer):
                def one(c, u, n):
                    early = isinstance(c, int) and layer == 0
                    pe.wait_ge(zn_ready, n + 1)
                    if not early or c >= 2:
                        pe.wait_ge(ht_ready, n - 1)
                    turn4(6 + u, zn[u]).then_inc(zn_turned, 1)
                    pe.wait_ge(ht_ready, n + 1)
                    for j in range(4):
                        if not early or c >= 1:
                            pe.wait_ge(qkv_stored, n * 4 + (j - 3))
                        mm(ps[:, j, 0:3 * D], ht[u][:, j * P:(j + 1) * P], wqkv_sb[:, :], start=True,
                           stop=True).then_inc(qkv_done, 1)
                n = layer * CHUNKS
                one(0, 0, n)
                one(1, 1, n + 1)
                with pe.Fori(1, CHUNKS // 2) as i:
                    one(i * 2, 0, i * 2 + n)
                    one(i * 2 + 1, 1, i * 2 + (n + 1))

            def turn(layer, name, par, G, count, first):
                if not first:
                    pe.wait_ge(turn_taken, count)
                if name in ("ctx0", "ctx1"):
                    pe.wait_ge(ct_ready, G * 2 + (1 if name == "ctx0" else 0))
                    turn4(7, ct[:, :]).then_inc(turned, 1)
                    return
                if name in ("k_early", "q_early"):
                    pe.wait_ge(kst_ready if name == "k_early" else qst_ready, G + 3)
                if name == "qm_late":
                    pe.wait_ge(neg_ready, G * 2 + 2)
                if name == "qm_early":
                    pe.wait_ge(neg_ready, G * 2 + 3)
                src, half = {"k_late": (kst, 1), "k_early": (kst, 0), "q_late": (qst[(par + 1) % 2], 1),
                             "q_early": (qst[par], 0), "qm_late": (qst[par], 1),
                             "qm_early": (qst[(par + 1) % 2], 0)}[name]
                dst = ps[:, 7, :].bitcast(BF16).rearrange("p (a n) -> p a n", a=2)
                for pair in range(2):
                    for t in range(4):
                        last = pe.transpose(dst[:, pair, t * P:(t + 1) * P],
                                            src[:, 4 * half + t, 2 * pair:2 * pair + 2, :], ident_b[:, :])
                last.then_inc(turned, 1)

            def body(layer, g, par, n):
                G = g + layer * GROUPS
                at = {s: (name, i) for i, (name, s) in enumerate(turns(n))}
                before = takes_before(g) + layer * TAKES_OF_LAYER
                attends, takes_max = 0 <= n < GROUPS, 0 <= n + 1 < GROUPS

                def score(s, u):
                    if n or s or u > 1 or layer:
                        pe.wait_ge(exp_done, G * 64 + (4 * s + u - 1))
                    mm(ps[:, u % 2, :], kpad[par][:, u, s % 8 * P:(s % 8 + 1) * P], qm[s // 8][:, u // 2, :],
                       start=True, stop=True).then_inc(s_filled, 1)

                def top(s, u):
                    half, kh, j = s // 8, s % 8 // 4, s % 4
                    if n >= 0 or s or layer:
                        pe.wait_ge(max_taken, G * 64 + (64 + 4 * s + u - 3))
                    mm(ps[:, 2 + u, :], q0[half][:, u // 2, j * P:(j + 1) * P],
                       kpad[(par + 1) % 2][:, u, kh * 512:kh * 512 + 512], start=True,
                       stop=True).then_inc(max_filled, 1)

                def weigh(s, G, par):
                    pe.wait_ge(exp_done, G * 64 + (4 * s + 4))
                    if s == 0:
                        pe.wait_ge(vst_ready, G + 1)
                    if s % 8 == 0 and (s or n or layer):
                        pe.wait_ge(ct_ready, G * 2 + s // 8)
                    for u in range(GH):
                        last = mm(ps[32 * u:32 * u + 32, 6, :], vst[par][:, s % 8, u, :], pbuf[:, s % 2, u, :],
                                  start=(s % 8 == 0), stop=(s % 8 == 7))
                    last.then_inc(pv_done, 1)

                for s in range(16 if n < GROUPS else 3):
                    if s in at:
                        turn(layer, at[s][0], par, G, before + (takes_upto(n, at[s][0]) - takes(at[s][0])),
                             n == -2 and at[s][1] == 0 and not layer)
                    if s == 0 and n > -2 and n < GROUPS:
                        pe.wait_ge(turn_taken, before)
                    if s == 4 and takes_max:
                        pe.wait_ge(turn_taken, before + takes_upto(n, "k_late"))
                    if s == 8 and takes_max:
                        pe.wait_ge(turn_taken, before + takes_upto(n, "q_late"))
                    if s == 8 and attends:
                        pe.wait_ge(turn_taken, before + takes_upto(n, "qm_late"))
                    order = ("s0", "m0", "s1", "m1", "m2", "s2", "m3", "s3")
                    for what in order:
                        if what[0] == "s" and attends:
                            score(s, int(what[1]))
                        if what[0] == "m" and takes_max:
                            top(s, int(what[1]))
                    if s == 0:
                        if n >= 1:
                            weigh(15, G - 1, (par + 1) % 2)
                    elif attends:
                        weigh(s - 1, G, par)

            def chain_parts(layer, c, par):
                n = layer * CHUNKS + c
                first = isinstance(c, int) and c == 0 and layer == 0

                def turn_cx():
                    pe.wait_ge(cbuf_ready, n + 1)
                    if not first:
                        pe.wait_ge(wt_ready, n)
                    turn4(7, cbuf).then_inc(cx_turned, 1)

                def project_out():
                    pe.wait_ge(cxt_ready, n + 1)
                    if not first:
                        pe.wait_ge(lm_ready, n)
                    for j in range(4):
                        last = mm(ps[:, 6, j * P:(j + 1) * P], cxt[:, j * P:(j + 1) * P], wo_sb[:, :], start=True,
                                  stop=True)
                    last.then_inc(wo_done, 1)

                def turn_zn2():
                    pe.wait_ge(zn2_ready, n + 1)
                    if not isinstance(c, int) or c >= 2:
                        pe.wait_ge(x_final, n - 1)
                    turn4(7, zn2).then_inc(zn2_turned, 1)

                def logits():
                    pe.wait_ge(mtf_ready, n + 1)
                    for j in range(4):
                        last = mm(ps[:, 6, j * EXPERTS:(j + 1) * EXPERTS], mtf[:, j * P:(j + 1) * P],
                                  wg_sb[:, :], start=True, stop=True)
                    last.then_inc(logits_done, 1)

                def turn_w():
                    pe.wait_ge(w_ready, n + 1)
                    pe.transpose(ps[0:32, 7, 0:P], gate[:, 7, :], ident).then_inc(w_turned, 1)
                return turn_cx, project_out, turn_zn2, logits, turn_w

            def turn_out(layer, c):
                n = layer * CHUNKS + c
                pe.wait_ge(tmp_added, n * 7 + 7)
                if isinstance(c, int) and c == CHUNKS - 1:
                    pe.wait_ge(x_final, n)
                elif isinstance(c, int) and c == CHUNKS - 2:
                    pe.wait_ge(wt_ready, n + 2)
                else:
                    pe.wait_ge(cxt_ready, n + 3)
                turn4(7, acc).then_inc(out_turned, 1)

            def experts(layer, c, par, at):
                n = layer * CHUNKS + c
                w1v = [w[:, :].rearrange("p (e f) -> p e f", e=EXPERTS) for w in w1p]

                def hidden(k):
                    if k == 0:
                        pe.wait_ge(mt_ready, n + 1)
                    if k >= 4 or not (isinstance(c, int) and c == 0 and layer == 0):
                        pe.wait_ge(gelu_done, n * 32 + (k - 3))
                    cut = slice(k % FB * P, (k % FB + 1) * P)
                    for i, (a, b) in enumerate(((0, 0), (0, 1), (1, 0))):
                        last = mm(ps[:, k % 4, :], w1v[a][:, k // FB, cut], mtp[b][par], start=(i == 0),
                                  stop=(i == 2))
                    last.then_inc(h_filled, 1)

                for k in range(EXPERTS * FB):
                    for f in at.get(k, ()):
                        f()
                    hidden(k)
                    if k >= 3:
                        down(n, k - 3, isinstance(c, int) and c == 0 and layer == 0)
                    elif not (isinstance(c, int) and c == 0):
                        down(n - 1, EXPERTS * FB - 3 + k, False)

            def down(n, k, first):
                e, f = k // FB, k % FB
                pe.wait_ge(hh_ready, n * 32 + (k + 1))
                pe.wait_ge(hl_odd if k % 2 else hl_even, n * 16 + (k // 2 + 1))
                if f == 0 and not (first and e < 2):
                    pe.wait_ge(tmp_ready, n * 8 + (e - 1))
                w2v = [w[:, :].rearrange("p (e f d) -> p e f d", e=EXPERTS, f=FB) for w in w2p]
                for i, (a, b) in enumerate(((0, 0), (0, 1), (1, 0))):
                    last = mm(ps[:, 4 + e % 2, :], w2v[a][:, e, f, :], hp[b][k % 4], start=(f == 0 and i == 0),
                              stop=(f == FB - 1 and i == 2))
                last.then_inc(down_done, 1)

            def mix(layer):
                for f in chain_parts(layer, 0, 0):
                    f()

                def one(c, par, before):
                    parts = chain_parts(layer, c + 1, (par + 1) % 2)
                    at = {1: (parts[0],), 3: (parts[1],), 11: (parts[2],), 14: (parts[3],), 24: (parts[4],)}
                    if before:
                        at[7] = (lambda: turn_out(layer, c - 1),)
                    experts(layer, c, par, at)
                one(0, 0, False)
                with pe.Fori(0, 3) as i:
                    one(i * 2 + 1, 1, True)
                    one(i * 2 + 2, 0, True)
                experts(layer, 7, 1, {7: (lambda: turn_out(layer, 6),)})
                for k in range(EXPERTS * FB - 3, EXPERTS * FB):
                    down((layer + 1) * CHUNKS - 1, k, False)
                turn_out(layer, 7)

            def retain():
                pe.wait_ge(x_final, CHUNKS)

                def turn_z(c, u, first=False):
                    pe.wait_ge(rz_ready, c + 1)
                    if not first:
                        pe.wait_ge(rzt_ready, c)
                    turn4(7, zn[u]).then_inc(rz_turned, 1)

                def products(c, u):
                    pe.wait_ge(rzt_ready, c + 1)
                    mm(ps[:, 0, :], rw_sb[:, 0:D], rzt[u], start=True, stop=True).then_inc(rq_done, 1)
                    mm(ps[:, 1, :], rw_sb[:, D:2 * D], rzt[u], start=True, stop=True).then_inc(rk_done, 1)
                    for b in range(BATCH):
                        last = mm(ps[:, 2 + b // 2, b % 2 * 256:b % 2 * 256 + 256], rzt[u][:, b * P:(b + 1) * P],
                                  rw_sb[:, 2 * D:4 * D], start=True, stop=True)
                    last.then_inc(rkv_done, 1)

                def step(c, u, first=False, last=False):
                    if not last:
                        turn_z(c + 1, 1 - u)
                    cuts = [slice(b * P, (b + 1) * P) for b in range(BATCH)]
                    pe.wait_ge(rq_ready, c + 1)
                    pe.wait_ge(rk_ready, c + 1)
                    if not first:
                        pe.wait_ge(ram_ready, c)
                    for cut in cuts:
                        end = mm(ps[:, 4, cut], rk[u][:, cut], rq[u][:, cut], start=True, stop=True)
                    end.then_inc(ra_done, 1)
                    pe.wait_ge(rkd_ready, c + 1)
                    pe.wait_ge(rv_ready, c + 1)
                    if not last:
                        products(c + 1, 1 - u)
                    if not first:
                        pe.wait_ge(state_ready, c)
                    for cut in cuts:
                        end = mm(ps[:, 6, cut], rkd[u][:, cut], rv[u][:, cut], start=True, stop=True)
                    end.then_inc(rst_done, 1)
                    pe.wait_ge(ram_ready, c + 1)
                    pe.wait_ge(rqd_ready, c + 1)
                    if not first:
                        pe.wait_ge(rx_done, c)
                    for cut in cuts:
                        mm(ps[:, 5, cut], ram[:, cut], rv[u][:, cut], start=True, stop=False)
                        end = mm(ps[:, 5, cut], rqd[u][:, cut], state[:, cut], start=False, stop=True)
                    end.then_inc(ro_done, 1)
                turn_z(0, 0, first=True)
                products(0, 0)
                step(0, 0, first=True)
                with pe.Fori(0, KT // 2 - 1) as i:
                    step(i * 2 + 1, 1)
                    step(i * 2 + 2, 0)
                step(KT - 1, 1, last=True)

            pe.wait_ge(consts_done, 1)
            for layer in range(2):
                project(layer)
                pe.wait_ge(qkv_stored, (layer + 1) * TILES)
                bodies(pe, lambda g, par, n: body(layer, g, par, n))
                mix(layer)
                if layer == 0:
                    retain()


def constants():
    import numpy as np
    i = np.arange(P, dtype=np.float64)
    t = np.zeros((P, C_END), np.float32)
    t[:, C_IDENT:C_IDENT + P] = np.eye(P)
    diff = i[None, :] - i[:, None]
    t[:, C_MASK:C_MASK + P] = np.where(diff >= 0, GAMMA ** np.maximum(diff, 0), 0.0)
    t[:, C_ROW:C_ROW + P] = GAMMA ** (i + 1)[None, :]
    t[:, C_COL] = GAMMA ** (P - 1 - i)
    t[:, C_RANK:C_RANK + EXPERTS] = EXPERTS - np.arange(EXPERTS)
    return t


def laid_out(L0_attn_x, L0_attn_weight_q, L0_attn_weight_k, L0_attn_weight_v, L0_attn_theta, L0_ffn_ln1_g,
             L0_ffn_ln1_b, L0_ffn_ln2_g, L0_ffn_ln2_b, L0_ffn_Wq, L0_ffn_Wk, L0_ffn_Wv, L0_ffn_Wo, L0_ffn_Wg,
             L0_ffn_W1, L0_ffn_b1, L0_ffn_W2, L0_ffn_b2):
    import numpy as np
    vectors = (L0_ffn_ln1_g, L0_ffn_ln1_b, L0_ffn_ln2_g, L0_ffn_ln2_b, L0_attn_theta)
    room = np.zeros((D, 3), np.float32)
    small = {"table": constants(), "cols": np.concatenate([np.stack(vectors, 1), room], 1),
             "wqkv": np.concatenate([L0_ffn_Wq, L0_ffn_Wk, L0_ffn_Wv], 1), "wo": L0_ffn_Wo, "wg": L0_ffn_Wg,
             "rw": np.concatenate([L0_attn_weight_q, L0_attn_weight_k, L0_attn_weight_v, L0_attn_weight_k], 1),
             "b1": L0_ffn_b1.reshape(EXPERTS * FB, P).T, "b2": L0_ffn_b2.T}
    return {"x": L0_attn_x.reshape(TILES, P, D).transpose(1, 0, 2).reshape(P, TILES * D),
            "small": np.concatenate([small[name] for name, _ in SMALL], 1),
            "w1": L0_ffn_W1.transpose(1, 0, 2),
            "w2": L0_ffn_W2.reshape(EXPERTS, FB, P, D).transpose(2, 0, 1, 3)}


def kernel(**inputs):
    import numpy as np
    import concourse.bacc as bacc
    from concourse.bass_utils import run_bass_kernel_spmd

    nc = bacc.Bacc("TRN2", target_bir_lowering=False, num_devices=1)
    arrays = laid_out(**{name: np.asarray(a) for name, a in inputs.items()})
    arrays = {name: np.ascontiguousarray(a) for name, a in arrays.items()}
    args = [nc.dram_tensor(f"in_{name}", a.shape, mybir.dt.from_np(a.dtype), kind="ExternalInput").ap()
            for name, a in arrays.items()]
    out = nc.dram_tensor("result", (P, TILES * D), F32, kind="ExternalOutput").ap()
    macaron(nc, *args, out)
    r = run_bass_kernel_spmd(nc, [{f"in_{name}": a for name, a in arrays.items()}], core_ids=[0])
    return r.results[0]["result"].reshape(P, TILES, D).transpose(1, 0, 2).reshape(BATCH, SEQ, D)
```

```python
from contextlib import ExitStack

import concourse.bass as bass
from concourse import mybir

ALU = mybir.AluOpType
ACT = mybir.ActivationFunctionType
F32 = mybir.dt.float32
F32R = mybir.dt.float32r
BF16 = mybir.dt.bfloat16
AX = mybir.AxisListType

P = 128
D = 128
BATCH, SEQ = 4, 1024
TOK = BATCH * SEQ
TILES = TOK // P
CHUNKS = TILES // 4
HEADS, DH = 16, 8
GH = 4
GROUPS = BATCH * HEADS // GH
KT = SEQ // P
ROWS = 64
EXPERTS, FF = 8, 512
FB = FF // P
BLOCKS = EXPERTS * FB
X_LOADS = 4
EARLY = CHUNKS // 2
LAG = 6
W_COLS = EXPERTS * FF + BLOCKS * D
W_PIECES = GROUPS
W_PIECE = W_COLS // W_PIECES
EPS = 1e-5
SCALE = float(DH) ** -0.5
GAMMA = 0.96875
Q_PARTS = (0, 0, 1, 1, 0, 2)
K_PARTS = (0, 1, 0, 1, 2, 0)
MAX_ROW = 8 * len(Q_PARTS)
C_IDENT, C_MASK, C_ROW, C_COL, C_RANK, C_END = 0, 128, 256, 384, 385, 393

SMALL = (("table", C_END), ("cols", 8), ("wqkv", 3 * D), ("wo", D), ("wg", EXPERTS), ("rw", 4 * D),
         ("b1", EXPERTS * FB), ("b2", EXPERTS))

TURNS = (("k_late", 0), ("ctx1", 2), ("q_late", 4), ("qm_late", 6), ("ctx0", 10), ("qm_early", 12),
         ("k_early", 13), ("q_early", 15))


def turns(g):
    there = {"k_late": 0 <= g + 1 < GROUPS, "ctx1": 0 <= g - 1, "q_late": 0 <= g + 1 < GROUPS,
             "qm_late": 0 <= g < GROUPS, "ctx0": 0 <= g < GROUPS, "qm_early": 0 <= g + 1 < GROUPS,
             "k_early": 0 <= g + 2 < GROUPS, "q_early": 0 <= g + 2 < GROUPS}
    return [(name, s) for name, s in TURNS if there[name]]


def takes(name):
    return 2 if name in ("k_early", "k_late") else 1


def takes_in(g):
    return sum(takes(name) for name, _ in turns(g))


BODIES = list(range(-2, GROUPS + 1))
TAKES_OF_LAYER = sum(takes_in(g) for g in BODIES)
TURNS_OF_LAYER = sum(len(turns(g)) for g in BODIES)
FULL = len(TURNS)
LOOPED = (1, 13)


def turns_before(g):
    if isinstance(g, int):
        return sum(len(turns(i)) for i in BODIES if i < g)
    return g * FULL + (turns_before(1) - FULL)


def takes_before(g):
    if isinstance(g, int):
        return sum(takes_in(i) for i in BODIES if i < g)
    return g * takes_in(1) + (takes_before(1) - takes_in(1))


def takes_upto(g, name):
    names = [other for other, _ in turns(g)]
    return sum(takes(other) for other in names[:names.index(name) + 1])


def projections(n):
    at = {s: [] for s in range(16)}
    for c in range(EARLY, CHUNKS if n == -1 else EARLY):
        first = 4 * (c - EARLY)
        at[first].append(("turn", c, 0))
        for j in range(4):
            at[first + min(j + 1, 3)].append(("tile", c, j))
    return at


def chain_banks(c):
    return (2, 3) if isinstance(c, int) and c == 0 else (7, 6)


def expert_at(k):
    blocks = k - (LAG + FB - 1)
    return blocks // FB if blocks % FB == 0 else None


def bodies(eng, emit):
    for g in (-2, -1, 0):
        emit(g, g % 2, g)
    with eng.Fori(0, (LOOPED[1] - LOOPED[0]) // 2) as i:
        emit(i * 2 + 1, 1, 1)
        emit(i * 2 + 2, 0, 2)
    for g in range(LOOPED[1], GROUPS + 1):
        emit(g, g % 2, g)


class Chain:

    def __init__(self, eng, sem, apart=None):
        self.eng, self.sem, self.n, self.base, self.apart = eng, sem, 0, 0, apart

    def link(self, ins):
        self.mark(ins)
        self.need()

    def mark(self, ins):
        self.n += 1
        ins.then_inc(self.sem, 1)

    def need(self):
        self.eng.wait_ge(self.sem, self.base + self.n)
        if self.apart and not isinstance(self.base, int):
            self.apart()

    def loop(self, i, per):
        self.start = self.n
        self.base = i * per

    def end(self, times, per):
        assert self.n == self.start + per, (self.n - self.start, per)
        self.n = self.start + times * per
        self.base = 0


def macaron(nc, x_in, small_in, w, out):
    with ExitStack() as ctx:
        def sb(name, shape, dt=F32):
            return ctx.enter_context(nc.sbuf_tensor(name, shape, dt))

        def sem(name):
            return ctx.enter_context(nc.semaphore(name))

        x = sb("x", [P, TILES * D])
        qkv = sb("qkv", [P, 3 * TILES * D])
        cx = qkv[:, 0:TILES * D]
        wp = [sb(f"wp{i}", [P, W_COLS], F32R) for i in range(2)]
        w1p = [half[:, 0:EXPERTS * FF] for half in wp]
        w2p = [half[:, EXPERTS * FF:W_COLS] for half in wp]
        w_piece = sb("w_piece", [P, W_PIECE])
        small = sb("small", [P, sum(w for _, w in SMALL)])
        at = dict(zip([name for name, _ in SMALL], [sum(w for _, w in SMALL[:i]) for i in range(len(SMALL))]))
        part = {name: small[:, at[name]:at[name] + w] for name, w in SMALL}
        wqkv_sb, wo_sb, wg_sb, rw_sb, b2_sb, tab = (part[n] for n in ("wqkv", "wo", "wg", "rw", "b2", "table"))
        b1_sb = part["b1"].rearrange("p (e f) -> p e f", e=EXPERTS)
        cols = part["cols"]
        ident_b = sb("ident_b", [P, P], BF16)
        st = sb("st", [P, TILES * 6])
        mean = sb("mean", [P, TILES])
        var = sb("var", [P, TILES])
        rstd = sb("rstd", [P, TILES])
        rstd2 = sb("rstd2", [P, TILES])
        shift = sb("shift", [P, TILES])
        sd = sb("sd", [P, TILES])
        ta = sb("ta", [P, TILES])
        tb = sb("tb", [P, TILES])
        gate = sb("gate", [P, 8, 32])
        gs = sb("gs", [P, 8, 4])
        st2 = sb("st2", [P, 4, 6])
        mv2 = sb("mv2", [P, 4, 2])
        ln2c = sb("ln2c", [P, 4, 4])
        wts_t = sb("wts_t", [32, P])[:, :]
        state = sb("state", [P, BATCH * D])
        with ExitStack() as phase:
            def at_(name, shape, dt=F32):
                return phase.enter_context(nc.sbuf_tensor(name, shape, dt))

            pbuf = at_("pbuf", [P, 2, GH, 512])
            q0 = [at_(f"q0{i}", [P, 2, 512], BF16) for i in range(2)]
            qm = [at_(f"qm{i}", [P, 2, 512], BF16) for i in range(2)]
            ct = at_("ct", [P, 512])
            rest = at_("rest", [P, 2, KT * GH * DH])
            nmax = at_("nmax", [P, 2, 2, 16])
            negm = at_("negm", [P, 16])
            negr = at_("negr", [P, 16])
            rden = at_("rden", [P, 16])
            qst, vst, kpad = [None] * 2, [None] * 2, [None] * 2
            for i in (1, 0):
                qst[i] = at_(f"qst{i}", [P, KT, GH, ROWS], BF16)
                vst[i] = at_(f"vst{i}", [P, KT, GH, 32])
                kpad[i] = at_(f"kpad{i}", [P, GH, SEQ], BF16)
            kst = at_("kst", [P, KT, GH, ROWS], BF16)
        with ExitStack() as phase:
            def at_(name, shape, dt=F32):
                return phase.enter_context(nc.sbuf_tensor(name, shape, dt))[:, :]

            hr = [at_(f"hr{i}", [P, 512]) for i in range(4)]
            hp = [[at_(f"hp{part}{i}", [P, 512], F32R) for i in range(8)] for part in range(2)]
            tmp = [at_(f"tmp{i}", [P, 512]) for i in range(2)]
            acc, *mtp_odd = (at_("acc", [P, 512]), at_("mtp01", [P, 512], F32R), at_("mtp11", [P, 512], F32R))
            mtp = [[at_(f"mtp{part}0", [P, 512], F32R), mtp_odd[part]] for part in range(2)]
            cbuf, cxt, x2, zn2, mtf = (at_(n, [P, 512]) for n in ("cbuf", "cxt", "x2", "zn2", "mtf"))
        with ExitStack() as phase:
            def at_(name, shape, dt=F32):
                return phase.enter_context(nc.sbuf_tensor(name, shape, dt))[:, :]

            zn = [at_(f"zn{i}", [P, 512]) for i in range(2)]
            ht = [at_(f"ht{i}", [P, 512]) for i in range(2)]
            rzt, rq, rk, rqd, rv, rkd = ([at_(f"{n}{i}", [P, 512]) for i in range(2)]
                                         for n in ("rzt", "rq", "rk", "rqd", "rv", "rkd"))
            ram = at_("ram", [P, 512])
        wbc = [qkv[:, 4096 * (i + 1):4096 * (i + 2)] for i in range(2)]
        w_dram = nc.dram_tensor("w_scratch", [2, 32, P], F32, kind="Internal").ap()

        ps = ctx.enter_context(nc.psum_tensor("ps", [P, 8, 512], F32))

        ident = tab[:, C_IDENT:C_IDENT + P]
        qkv5 = qkv[:, :].rearrange("p (a h n) -> p a h n", a=3, h=4)

        x_loaded = [sem(f"x_loaded{i}") for i in range(X_LOADS)]
        small_loaded, w_loaded, w_split, w_rest = (
            sem("small_loaded"), sem("w_loaded"), sem("w_split"), sem("w_rest"))
        consts_done, theta_z, theta_e = sem("consts_done"), sem("theta_z"), sem("theta_e")
        stats_done, var_ready, sd_ready, norm_ready = (sem("stats_done"), sem("var_ready"),
                                                       sem("sd_ready"), sem("norm_ready"))
        dve_seq, pool_seq = sem("dve_seq"), sem("pool_seq")
        zn_ready, zn_turned, ht_ready, qkv_done, qkv_stored = (
            sem("zn_ready"), sem("zn_turned"), sem("ht_ready"), sem("qkv_done"), sem("qkv_stored"))
        stacks_clear = sem("stacks_clear")
        kst_ready, qst_ready, vst_ready = sem("kst_ready"), sem("qst_ready"), sem("vst_ready")
        turned, turn_taken = sem("turned"), sem("turn_taken")
        max_filled, max_taken = sem("max_filled"), sem("max_taken")
        neg_ready = sem("neg_ready")
        s_filled, exp_done, pv_done, ct_ready = sem("s_filled"), sem("exp_done"), sem("pv_done"), sem("ct_ready")
        cbuf_ready, cx_turned, cxt_ready, wo_done, x2_ready, var2_ready, sd2_ready, norm2_ready = (
            sem("cbuf_ready"), sem("cx_turned"), sem("cxt_ready"), sem("wo_done"), sem("x2_ready"),
            sem("var2_ready"), sem("sd2_ready"), sem("norm2_ready"))
        zn2_ready, zn2_turned, mt_ready, logits_done, lm_ready, ex_ready, w_ready, w_turned, wt_ready = (
            sem("zn2_ready"), sem("zn2_turned"), sem("mt_ready"), sem("logits_done"), sem("lm_ready"),
            sem("ex_ready"), sem("w_ready"), sem("w_turned"), sem("wt_ready"))
        w_written, w_spread = sem("w_written"), sem("w_spread")
        mtf_ready, down_done, hh_ready, hl_even, hl_odd = (sem("mtf_ready"), sem("down_done"), sem("hh_ready"),
                                                           sem("hl_even"), sem("hl_odd"))
        h_filled, gelu_done, tmp_ready, tmp_added, out_turned, x_final = (
            sem("h_filled"), sem("gelu_done"), sem("tmp_ready"), sem("tmp_added"), sem("out_turned"),
            sem("x_final"))
        rz_ready, rz_turned, rzt_ready, rq_done, rk_done, rkv_done, rq_ready, rk_ready = (
            sem("rz_ready"), sem("rz_turned"), sem("rzt_ready"), sem("rq_done"), sem("rk_done"),
            sem("rkv_done"), sem("rq_ready"), sem("rk_ready"))
        rkd_ready, rv_ready, rqd_ready, ra_done, ram_ready, ro_done, rst_done, rx_done, state_ready = (
            sem("rkd_ready"), sem("rv_ready"), sem("rqd_ready"), sem("ra_done"), sem("ram_ready"),
            sem("ro_done"), sem("rst_done"), sem("rx_done"), sem("state_ready"))
        stored = sem("stored")

        block = ctx.enter_context(nc.Block())

        def group_view(a, g):
            return qkv[:, bass.ds(g * 256 + a * TILES * D, 256)].rearrange(
                "p (t h d) -> p t h d", t=KT, h=GH)

        def parts(eng, chain, room, a, g, dst, order):
            src = group_view(a, g)
            r = [room[:, i, :].rearrange("p (t h d) -> p t h d", t=KT, h=GH) for i in range(2)]

            def rows(j):
                return dst[:, :, :, 8 * j:8 * j + 8]

            level = [[j for j, part in enumerate(order) if part == n] for n in range(3)]
            for j in level[0][1:]:
                eng.tensor_copy(rows(j), src)
            chain.link(eng.tensor_copy(rows(level[0][0]), src))
            chain.link(eng.tensor_tensor(r[0], src, rows(level[0][0]), ALU.subtract))
            for j in level[1][1:]:
                eng.tensor_copy(rows(j), r[0])
            chain.link(eng.tensor_copy(rows(level[1][0]), r[0]))
            chain.link(eng.tensor_tensor(r[1], r[0], rows(level[1][0]), ALU.subtract))
            return eng.tensor_copy(rows(level[2][0]), r[1])

        @block.sync
        def _(sp):
            width = TILES * D // X_LOADS
            for i in range(X_LOADS):
                cut = slice(i * width, (i + 1) * width)
                sp.dma_start(x[:, cut], x_in[:, cut]).then_inc(x_loaded[i], 16)
            sp.dma_start(small[:, :], small_in).then_inc(small_loaded, 16)
            sp.dma_start(w_piece[:, :], w[:, 0:W_PIECE]).then_inc(w_loaded, 16)
            with sp.Fori(1, W_PIECES) as i:
                sp.wait_ge(w_rest, i)
                sp.dma_start(w_piece[:, :], w[:, bass.ds(i * W_PIECE, W_PIECE)]).then_inc(w_loaded, 16)

            def spread(layer, c, par):
                n = layer * CHUNKS + c
                sp.wait_ge(wt_ready, n + 1)
                sp.dma_start(w_dram[par], wts_t).then_inc(w_written, 16)
                sp.wait_ge(w_written, n * 16 + 16)
                if not (isinstance(c, int) and layer == 0 and c < 2):
                    sp.wait_ge(tmp_ready, n * 8 - 8)
                sp.dma_start(wbc[par], w_dram[par].rearrange("r t -> (r t)").partition_broadcast(P)
                             ).then_inc(w_spread, 16)

            def store(c):
                sp.wait_ge(x_final, CHUNKS + c + 1)
                cut = bass.ds(c * 512, 512)
                sp.dma_start(out[:, cut], x[:, cut]).then_inc(stored, 16)

            for layer in range(2):
                spread(layer, 0, 0)
                spread(layer, 1, 1)
                with sp.Fori(1, 4) as i:
                    for u in range(2):
                        if layer == 1:
                            store(i * 2 + (u - 2))
                        spread(layer, i * 2 + u, u)
            store(6)
            store(7)
            sp.wait_ge(stored, 16 * CHUNKS)

        @block.gpsimd
        def _(pool):
            def apart():
                pool.nop(nofuse=True)

            chain = Chain(pool, pool_seq, apart)
            def constant_parts():
                for i in range(2):
                    pool.memset(kpad[i][:, :, :].bitcast(F32), 0.0)
                    pool.memset(vst[i][:, :, :, :], 0.0)
                    pool.memset(qst[i][:, :, :, :].bitcast(F32), 0.0)
                chain.link(pool.memset(kst[:, :, :, :].bitcast(F32), 0.0))
                pool.memset(kst[:, :, :, MAX_ROW:MAX_ROW + 3], 1.0)
                for i in range(2):
                    last = pool.memset(vst[i][:, :, :, DH:DH + 1], 1.0)
                chain.link(last)
                pool.nop(nofuse=True).then_inc(stacks_clear, 1)

            def body(layer, g, par, n):
                at = dict((name, i) for i, (name, _) in enumerate(turns(n)))
                before = turns_before(g) + layer * TURNS_OF_LAYER
                G = g + layer * GROUPS
                if 0 <= n + 1 < GROUPS:
                    if n >= 1 or layer:
                        pool.wait_ge(ct_ready, G * 2)
                        apart()
                    pool.tensor_copy(vst[(par + 1) % 2][:, :, :, 0:DH],
                                     group_view(2, g + 1)).then_inc(vst_ready, 1)
                if 1 <= n + 2 < GROUPS:
                    pool.wait_ge(turned, before + at["k_late"] + 1)
                    apart()
                    parts(pool, chain, rest, 1, g + 2, kst, K_PARTS).then_inc(kst_ready, 1)
                    if n >= 0:
                        pool.wait_ge(turned, before + at["qm_late"] + 1)
                        apart()
                    chain.link(pool.memset(qst[par][:, :, :, MAX_ROW:MAX_ROW + 3], 0.0))
                    parts(pool, chain, rest, 0, g + 2, qst[par], Q_PARTS).then_inc(qst_ready, 1)

            def attend(layer):
                constant_parts()
                pool.wait_ge(qkv_stored, layer * TILES + 2 * KT)
                body(layer, -1, 1, -1)
                pool.wait_ge(qkv_stored, (layer + 1) * TILES)
                body(layer, 0, 0, 0)
                with pool.Fori(0, 6) as i:
                    chain.loop(i, 18)
                    body(layer, i * 2 + 1, 1, 1)
                    body(layer, i * 2 + 2, 0, 2)
                    chain.end(6, 18)
                for g in range(13, GROUPS):
                    body(layer, g, g % 2, g)
                gather_cx(layer, 0)
                gather_cx(layer, 1)

            def gather_cx(layer, c):
                n = layer * CHUNKS + c
                if isinstance(c, int) and c == 0:
                    pool.wait_ge(pv_done, (layer * GROUPS + GROUPS - 1) * 16)
                if not isinstance(c, int) or c or layer:
                    pool.wait_ge(cx_turned, n)
                    apart()
                pool.tensor_copy(cbuf.rearrange("p (t h n) -> p h t n", t=4, h=4),
                                 cx.rearrange("p (h n) -> p h n", h=4)[:, :, bass.ds(c * 128, 128)]
                                 .rearrange("p h (t n) -> p h t n", t=4)).then_inc(cbuf_ready, 1)

            def sum_experts(layer, c, gathers=True):
                n = layer * CHUNKS + c
                first = isinstance(c, int) and c == 0 and layer == 0
                for k in range(1, BLOCKS, 2):
                    pool.wait_ge(hh_ready, n * 32 + (k + 1))
                    pool.tensor_tensor(hp[1][k % 8], hr[k % 4], hp[0][k % 8].bitcast(F32),
                                       ALU.subtract).then_inc(hl_odd, 1)
                    e = expert_at(k)
                    if e is not None and e >= 1:
                        add_expert(n, e, first)
                    elif e is not None and e < 0 and not (isinstance(c, int) and c == 0):
                        add_expert(n - 1, e + EXPERTS, False)
                    if k == 17 and gathers:
                        gather_cx(layer, c + 2)

            def add_expert(n, e, first):
                pool.wait_ge(tmp_ready, n * 8 + (e + 1))
                if e == 1:
                    if not first:
                        pool.wait_ge(out_turned, n)
                    ins = pool.tensor_tensor(acc, tmp[0], tmp[1], ALU.add)
                else:
                    pool.wait_ge(tmp_added, n * 7 + (e - 1))
                    ins = pool.tensor_tensor(acc, acc, tmp[e % 2], ALU.add)
                ins.then_inc(tmp_added, 1)

            def mix(layer):
                pool.wait_ge(turn_taken, (layer + 1) * TAKES_OF_LAYER)
                sum_experts(layer, 0)
                with pool.Fori(1, CHUNKS - 2) as c:
                    sum_experts(layer, c)
                for c in (CHUNKS - 2, CHUNKS - 1):
                    sum_experts(layer, c, gathers=False)
                for e in (EXPERTS - 2, EXPERTS - 1):
                    add_expert((layer + 1) * CHUNKS - 1, e, False)

            def retain():
                def one(c, u):
                    pool.wait_ge(rq_ready, c + 1)
                    pool.tensor_tensor(rqd[u].rearrange("p (b t) -> p b t", b=BATCH),
                                       rq[u].rearrange("p (b t) -> p b t", b=BATCH),
                                       tab[:, C_ROW:C_ROW + P].unsqueeze(1).broadcast_to([P, BATCH, P]),
                                       ALU.mult).then_inc(rqd_ready, 1)
                with pool.Fori(0, KT // 2) as i:
                    one(i * 2, 0)
                    one(i * 2 + 1, 1)
                pool.wait_ge(rx_done, KT)

            pool.memset(state[:, :], 0.0)
            pool.wait_ge(small_loaded, 16)
            for layer in range(2):
                attend(layer)
                mix(layer)
                if layer == 0:
                    retain()

        @block.scalar
        def _(act):
            def std(n):
                act.wait_ge(var_ready, n)
                act.activation(sd[:, :], ta[:, :], ACT.Sqrt).then_inc(sd_ready, 1)

            def normed(dst, c, n):
                if not isinstance(c, int) or n > 1:
                    act.wait_ge(zn_turned, n - 1)
                for j in range(4):
                    t = c * 4 + j
                    last = act.activation(dst[:, j * D:(j + 1) * D], x[:, bass.ds(t * D, D)], ACT.Identity,
                                          scale=rstd2[:, bass.ds(t, 1)], bias=shift[:, bass.ds(t, 1)])
                last.then_inc(zn_ready, 1)

            def keep_qkv(layer, t, bank):
                act.wait_ge(qkv_done, layer * TILES + t + 1)
                act.activation(qkv5[:, :, :, bass.ds(t * 32, 32)],
                               ps[:, bank, 0:3 * D].rearrange("p (a h n) -> p a h n", a=3, h=4),
                               ACT.Copy).then_inc(qkv_stored, 1)

            def project(layer):
                n = layer * CHUNKS
                std(3 * layer + 1)
                std(3 * layer + 2)
                act.wait_ge(norm_ready, 2 * layer + 1)
                normed(zn[0], 0, n)
                normed(zn[1], 1, n + 1)
                for c in range(EARLY):
                    for j in range(4):
                        keep_qkv(layer, c * 4 + j, j)
                    if c < EARLY - 1:
                        normed(zn[c % 2], c + 2, n + c + 2)

            def take_turn(name, par, count, both):
                act.wait_ge(turned, count)
                src = ps[:, 7, :].bitcast(BF16).rearrange("p (a n) -> p a n", a=2)
                if name in ("k_early", "k_late"):
                    kh = 512 * (name == "k_late")
                    k2 = (par + (name == "k_late")) % 2
                    if both:
                        act.activation(kpad[k2][64:128, 1:GH:2, kh:kh + 512], src[64:128, :, :],
                                       ACT.Copy).then_inc(turn_taken, 1)
                    last = act.activation(kpad[k2][0:64, 0:GH:2, kh:kh + 512], src[0:64, :, :], ACT.Copy)
                else:
                    dst = {"q_early": q0[0], "q_late": q0[1], "qm_early": qm[0], "qm_late": qm[1]}[name]
                    last = act.activation(dst[:, :, :], src, ACT.Copy)
                last.then_inc(turn_taken, 1)

            def body(layer, g, par, n):
                G = g + layer * GROUPS
                at = {s: (name, i) for i, (name, s) in enumerate(turns(n))}
                before = turns_before(g) + layer * TURNS_OF_LAYER
                aside = dict(zip((2, 5, 6, 8, 11), chain_parts(layer, 0))) if n == GROUPS - 1 else {}
                projects = projections(n)
                banks = (0, 1, 4, 5) if n == GROUPS - 1 else (0, 1, 0, 1)

                def between(s):
                    if s in aside:
                        aside[s]()
                    if (s == 1 and n >= 1) or (s == 9 and 0 <= n < GROUPS):
                        act.wait_ge(pv_done, G * 16 + (s - 1))
                        act.activation(ct[:, :], ps[:, 6, :], ACT.Copy).then_inc(ct_ready, 1)
                    if s == 5 and layer == 0 and -1 <= n < GROUPS - 1:
                        act.wait_ge(w_loaded, g * 16 + 32)
                        act.activation(wp[0][:, bass.ds((g + 1) * W_PIECE, W_PIECE)], w_piece[:, :],
                                       ACT.Copy).then_inc(w_split, 1)
                    if s in at and not at[s][0].startswith("ctx"):
                        take_turn(at[s][0], par, before + (at[s][1] + 1), n == -1)

                for s in range(16 if n < GROUPS else 3):
                    if 0 <= n < GROUPS:
                        for u in range(GH):
                            if u == 2:
                                between(s)
                            act.wait_ge(s_filled, G * 64 + (4 * s + u + 1))
                            if u == 0 and (n > 0 or s > 1 or layer):
                                act.wait_ge(pv_done, G * 16 + (s - 1))
                            act.activation(pbuf[:, s % 2, u, :], ps[:, banks[u], :], ACT.Exp,
                                           scale=SCALE).then_inc(exp_done, 1)
                    else:
                        between(s)
                    for what, c, j in projects[s]:
                        if what == "turn":
                            act.wait_ge(zn_turned, layer * CHUNKS + c + 1)
                            act.activation(ht[c % 2], ps[:, 6, :], ACT.Identity, scale=cols[:, 0:1],
                                           bias=cols[:, 1:2]).then_inc(ht_ready, 1)
                            if c == EARLY:
                                normed(zn[(c + 1) % 2], c + 1, layer * CHUNKS + c + 1)
                        else:
                            keep_qkv(layer, c * 4 + j, j % 2)
                            if j == 3 and c + 2 < CHUNKS:
                                normed(zn[c % 2], c + 2, layer * CHUNKS + c + 2)

            def gelus(layer, c, after):
                n = layer * CHUNKS + c
                for k in range(BLOCKS):
                    act.wait_ge(h_filled, n * 32 + (k + 1))
                    if k >= 4 or not (isinstance(c, int) and c == 0 and layer == 0):
                        act.wait_ge(hh_ready, n * 32 + (k - 3))
                        act.wait_ge(hl_odd if k % 2 else hl_even, n * 16 + (k // 2 - 1))
                    act.activation(hr[k % 4], ps[:, k % 4, :], ACT.Gelu_apprx_tanh,
                                   bias=b1_sb[:, k // 4, k % 4:k % 4 + 1]).then_inc(gelu_done, 1)
                    for f in after.get(k, ()):
                        f()

            def chain_parts(layer, c):
                n = layer * CHUNKS + c
                bank = chain_banks(c)[0]

                def copy_cx():
                    act.wait_ge(cx_turned, n + 1)
                    act.activation(cxt, ps[:, bank, :], ACT.Copy).then_inc(cxt_ready, 1)

                def root():
                    act.wait_ge(var2_ready, n + 1)
                    act.activation(ln2c[:, 1, :], ln2c[:, 0, :], ACT.Sqrt).then_inc(sd2_ready, 1)

                def norm():
                    act.wait_ge(norm2_ready, n + 1)
                    for j in range(4):
                        last = act.activation(zn2[:, j * D:(j + 1) * D], x2[:, j * D:(j + 1) * D], ACT.Identity,
                                              scale=ln2c[:, 2, j:j + 1], bias=ln2c[:, 3, j:j + 1])
                    last.then_inc(zn2_ready, 1)

                def affine():
                    act.wait_ge(zn2_turned, n + 1)
                    act.activation(mtf, ps[:, bank, :], ACT.Identity, scale=cols[:, 2:3],
                                   bias=cols[:, 3:4]).then_inc(mtf_ready, 1)

                def expo():
                    act.wait_ge(lm_ready, n + 1)
                    act.activation(gate[:, 1, :], gate[:, 0, :], ACT.Exp).then_inc(ex_ready, 1)
                return copy_cx, root, norm, affine, expo

            def mix(layer):
                def one(c):
                    copy_cx, root, norm, affine, expo = chain_parts(layer, c + 1)
                    gelus(layer, c, {2: (copy_cx,), 8: (root,), 10: (norm,), 15: (affine,), 19: (expo,)})
                one(0)
                with act.Fori(1, CHUNKS - 1) as c:
                    one(c)
                gelus(layer, CHUNKS - 1, {})

            def retain():
                act.wait_ge(theta_z, 1)
                act.activation(cols[:, 6:7], cols[:, 5:6], ACT.Exp).then_inc(theta_e, 1)
                std(3)
                act.wait_ge(norm_ready, 2)
                act.wait_ge(theta_e, 2)

                def normed_x(c, u, first):
                    if not first:
                        act.wait_ge(rz_turned, c - 1)
                    for b in range(BATCH):
                        t = c + b * KT
                        last = act.activation(zn[u][:, b * D:(b + 1) * D], x[:, bass.ds(t * D, D)], ACT.Identity,
                                              scale=rstd[:, bass.ds(t, 1)], bias=shift[:, bass.ds(t, 1)])
                    last.then_inc(rz_ready, 1)

                def operands(c, u, first):
                    if not first:
                        act.wait_ge(ro_done, c - 1)
                    act.wait_ge(rq_done, c + 1)
                    act.activation(rq[u], ps[:, 0, :], ACT.Copy, scale=cols[:, 7:8]).then_inc(rq_ready, 1)
                    act.wait_ge(rk_done, c + 1)
                    act.activation(rk[u], ps[:, 1, :], ACT.Copy).then_inc(rk_ready, 1)
                    act.wait_ge(rkv_done, c + 1)
                    act.activation(rkd[u].rearrange("p (b d) -> p b d", b=BATCH),
                                   ps[:, 2:4, :].rearrange("p a (b n) -> p (a b) n", b=2)[:, :, D:2 * D],
                                   ACT.Copy, scale=tab[:, C_COL:C_COL + 1]).then_inc(rkd_ready, 1)
                normed_x(0, 0, True)
                normed_x(1, 1, True)
                operands(0, 0, True)
                normed_x(2, 0, False)
                operands(1, 1, True)
                normed_x(3, 1, False)
                with act.Fori(1, KT // 2 - 1) as i:
                    for u in range(2):
                        operands(i * 2 + u, u, False)
                        normed_x(i * 2 + (u + 2), u, False)
                operands(KT - 2, 0, False)
                operands(KT - 1, 1, False)

            act.wait_ge(small_loaded, 16)
            for layer in range(2):
                project(layer)
                bodies(act, lambda g, par, n: body(layer, g, par, n))
                mix(layer)
                if layer == 0:
                    retain()

        @block.vector
        def _(dve):
            chain = Chain(dve, dve_seq)

            def tile_stats(t):
                dve.bn_stats(st[:, bass.ds(t * 6, 6)], x[:, bass.ds(t * D, D)]).then_inc(stats_done, 1)

            def stats(n):
                dve.wait_ge(stats_done, TILES * (n + 1))
                s = st[:, :].rearrange("p (t c) -> p t c", c=6)
                dve.tensor_tensor(ta[:, :], s[:, :, 1], s[:, :, 4], ALU.subtract)
                dve.tensor_tensor(tb[:, :], s[:, :, 2], s[:, :, 5], ALU.add)
                chain.link(dve.tensor_tensor(mean[:, :], s[:, :, 1], s[:, :, 4], ALU.add))
                dve.tensor_scalar(mean[:, :], mean[:, :], 0.5, None, ALU.mult)
                dve.tensor_scalar(tb[:, :], tb[:, :], 1.0 / D, None, ALU.mult)
                chain.link(dve.tensor_tensor(ta[:, :], ta[:, :], ta[:, :], ALU.mult))
                chain.link(dve.scalar_tensor_tensor(out=var[:, :], in0=ta[:, :], scalar=0.25, in1=tb[:, :],
                                                    op0=ALU.mult, op1=ALU.add))
                dve.tensor_scalar(ta[:, :], var[:, :], EPS, None, ALU.add).then_inc(var_ready, 1)

            def ht_evac(bank, u, n):
                dve.wait_ge(zn_turned, n + 1)
                dve.tensor_scalar(ht[u], ps[:, bank, :], cols[:, 0:1], cols[:, 1:2], ALU.mult,
                                  ALU.add).then_inc(ht_ready, 1)

            def project(layer):
                if layer == 0:
                    for i in range(X_LOADS):
                        dve.wait_ge(x_loaded[i], 16)
                        for t in range(i * TILES // X_LOADS, (i + 1) * TILES // X_LOADS):
                            tile_stats(t)
                stats(2 * layer)
                if layer == 0:
                    dve.wait_ge(small_loaded, 16)
                    dve.tensor_copy(ident_b[:, :], ident).then_inc(consts_done, 1)
                dve.wait_ge(sd_ready, 3 * layer + 1)
                chain.link(dve.reciprocal(rstd[:, :], sd[:, :]))
                chain.link(dve.tensor_tensor(tb[:, :], rstd[:, :], rstd[:, :], ALU.mult))
                chain.link(dve.tensor_tensor(tb[:, :], tb[:, :], var[:, :], ALU.mult))
                dve.tensor_scalar(ta[:, :], tb[:, :], EPS, None, ALU.add).then_inc(var_ready, 1)
                dve.wait_ge(sd_ready, 3 * layer + 2)
                chain.link(dve.reciprocal(rstd2[:, :], sd[:, :]))
                chain.link(dve.tensor_tensor(rstd2[:, :], rstd2[:, :], rstd[:, :], ALU.mult))
                dve.scalar_tensor_tensor(out=shift[:, :], in0=mean[:, :], scalar=-1.0, in1=rstd2[:, :],
                                         op0=ALU.mult, op1=ALU.mult).then_inc(norm_ready, 1)
                for c in range(EARLY - 1):
                    ht_evac(6 + c % 2, c % 2, layer * CHUNKS + c)
                dve.wait_ge(stacks_clear, layer + 1)
                dve.wait_ge(qkv_stored, layer * TILES + KT)
                room = ct[:, :].rearrange("p (i n) -> p i n", i=2)
                parts(dve, chain, room, 1, 0, kst, K_PARTS).then_inc(kst_ready, 1)
                ht_evac(6 + (EARLY - 1) % 2, (EARLY - 1) % 2, layer * CHUNKS + EARLY - 1)
                parts(dve, chain, room, 0, 0, qst[0], Q_PARTS).then_inc(qst_ready, 1)

            def neg_step(layer, g, par, half, k):
                col = qst[par][:, 4 * half:4 * half + 4, :, :]
                a = negm[:, :].rearrange("p (t h) -> p t h", t=4)
                r = negr[:, :].rearrange("p (t h) -> p t h", t=4)
                part = [col[:, :, :, MAX_ROW + i] for i in range(3)]
                if k == 0:
                    link = dve.tensor_tensor(negm[:, :], nmax[:, half, 0, :], nmax[:, half, 1, :], ALU.min)
                elif k == 1:
                    link = dve.tensor_copy(part[0], a)
                elif k == 2:
                    link = dve.tensor_tensor(r, a, part[0], ALU.subtract)
                elif k == 3:
                    link = dve.tensor_copy(part[1], r)
                elif k == 4:
                    link = dve.tensor_tensor(a, r, part[1], ALU.subtract)
                else:
                    dve.tensor_copy(part[2], a).then_inc(neg_ready, 1)
                    return
                chain.mark(link)

            def body(layer, g, par, n):
                G = g + layer * GROUPS
                at = {s: (name, i) for i, (name, s) in enumerate(turns(n))}
                before = turns_before(g) + layer * TURNS_OF_LAYER
                aside = {}
                if n == GROUPS - 1:
                    aside = dict(zip((3, 4, 6, 8, 9, 11, 12, 13, 14, 15), chain_parts(layer, 0, 0)))
                steps = []

                def next_step():
                    if steps:
                        half, k = steps.pop(0)
                        if k == 0:
                            dve.wait_ge(max_taken, (G + 1) * 64 + (0 if half else 32))
                        else:
                            chain.need()
                        neg_step(layer, g if half else g + 1, par if half else (par + 1) % 2, half, k)

                for s in range(16 if n < GROUPS else 3):
                    half, kh, j = s // 8, s % 8 // 4, s % 4
                    if s == 0 and 0 <= n < GROUPS:
                        steps += [(1, k) for k in range(6)]
                    if s == 8 and 0 <= n + 1 < GROUPS:
                        steps += [(0, k) for k in range(6)]
                    for u in range(0, GH, 2):
                        next_step()
                        if 0 <= n + 1 < GROUPS:
                            dve.wait_ge(max_filled, (G + 1) * 64 + (4 * s + u + 2))
                            dve.tensor_reduce(nmax[:, half, kh, 4 * j + u:4 * j + u + 2], ps[:, 2 + u:4 + u, :],
                                              AX.X, ALU.max, negate=True).then_inc(max_taken, 2)
                        if u == 0 and n != -1 and s in at and at[s][0] in ("k_early", "k_late"):
                            name, i = at[s]
                            late = name == "k_late"
                            dve.wait_ge(turned, before + i + 1)
                            src = ps[:, 7, :].bitcast(BF16).rearrange("p (a n) -> p a n", a=2)
                            dve.tensor_copy(kpad[(par + late) % 2][64:128, 1:GH:2, 512 * late:512 * late + 512],
                                            src[64:128, :, :]).then_inc(turn_taken, 1)
                    if s == 7 and layer == 0 and -1 <= n < GROUPS - 1:
                        dve.wait_ge(w_split, g + 2)
                        cut = bass.ds((g + 1) * W_PIECE, W_PIECE)
                        dve.tensor_tensor(wp[1][:, cut], w_piece[:, :], wp[0][:, cut].bitcast(F32),
                                          ALU.subtract).then_inc(w_rest, 1)
                    if s in aside:
                        aside[s]()
                    if s in at and at[s][0].startswith("ctx"):
                        name, i = at[s]
                        half_done = 1 if name == "ctx1" else 0
                        dve.wait_ge(turned, before + i + 1)
                        src = ps[:, 7, :].rearrange("p (t h n) -> p t h n", t=4, h=GH)
                        rd = rden[:, :].rearrange("p (t h) -> p t h", t=4)
                        chain.link(dve.reciprocal(rd, src[:, :, :, DH]))
                        g2 = g if name == "ctx0" else g - 1
                        dve.tensor_tensor(
                            cx[:, bass.ds(g2 * 256 + half_done * 128, 128)].rearrange(
                                "p (t h n) -> p t h n", t=4, h=GH),
                            src[:, :, :, 0:DH], rd.unsqueeze(3).broadcast_to([P, 4, GH, DH]),
                            ALU.mult).then_inc(turn_taken, 1)

            def attend(layer):
                for g in (-2, -1, 0):
                    body(layer, g, g % 2, g)
                with dve.Fori(0, 6) as i:
                    chain.loop(i, 24)
                    body(layer, i * 2 + 1, 1, 1)
                    body(layer, i * 2 + 2, 0, 2)
                    chain.end(6, 24)
                for g in range(13, GROUPS + 1):
                    body(layer, g, g % 2, g)

            g3 = [gate[:, i, :].rearrange("p (t e) -> p t e", t=4) for i in range(8)]
            rank = tab[:, C_RANK:C_RANK + EXPERTS].unsqueeze(1).broadcast_to([P, 4, EXPERTS])

            def bc(i):
                return gs[:, i, :].unsqueeze(2).broadcast_to([P, 4, EXPERTS])

            def chain_parts(layer, c, par):
                n = layer * CHUNKS + c
                bank, products = chain_banks(c)

                def recompute():
                    if not (isinstance(c, int) and c == 0 and layer == 0):
                        dve.wait_ge(zn2_ready, n)
                    for j in range(4):
                        t = c * 4 + j
                        last = dve.tensor_scalar(x2[:, j * D:(j + 1) * D], x[:, bass.ds(t * D, D)],
                                                 mean[:, bass.ds(t, 1)], rstd[:, bass.ds(t, 1)],
                                                 ALU.subtract, ALU.mult)
                    chain.mark(last)

                def residual():
                    chain.need()
                    dve.wait_ge(wo_done, n + 1)
                    xs = x[:, bass.ds(c * 512, 512)]
                    chain.link(dve.tensor_tensor(x2, ps[:, products, :], x2, ALU.add))
                    for j in range(4):
                        last = dve.bn_stats(st2[:, j, :], x2[:, j * D:(j + 1) * D])
                    chain.link(last)
                    dve.nop(nofuse=True)
                    for j in range(4):
                        last = dve.bn_aggr(mv2[:, j, :], st2[:, j, :])
                    chain.link(last)
                    dve.tensor_scalar(ln2c[:, 0, :], mv2[:, :, 1], EPS, None, ALU.add).then_inc(var2_ready, 1)
                    dve.scalar_tensor_tensor(out=xs, in0=x2, scalar=0.5, in1=xs, op0=ALU.mult,
                                             op1=ALU.add).then_inc(x2_ready, 1)

                def shift2():
                    dve.wait_ge(sd2_ready, n + 1)
                    chain.link(dve.reciprocal(ln2c[:, 2, :], ln2c[:, 1, :]))
                    dve.scalar_tensor_tensor(out=ln2c[:, 3, :], in0=mv2[:, :, 0], scalar=-1.0, in1=ln2c[:, 2, :],
                                             op0=ALU.mult, op1=ALU.mult).then_inc(norm2_ready, 1)

                def split_m():
                    dve.wait_ge(mtf_ready, n + 1)
                    chain.link(dve.tensor_copy(mtp[0][par], mtf))
                    dve.tensor_tensor(mtp[1][par], mtf, mtp[0][par].bitcast(F32),
                                      ALU.subtract).then_inc(mt_ready, 1)

                def gate1():
                    dve.wait_ge(logits_done, n + 1)
                    lg = ps[:, products, 0:32].rearrange("p (t e) -> p t e", t=4)
                    chain.link(dve.tensor_reduce(gs[:, 0, :], lg, AX.X, ALU.max))
                    dve.tensor_tensor(g3[0], lg, bc(0), ALU.subtract).then_inc(lm_ready, 1)

                def top(src, value, onehot):
                    chain.link(dve.tensor_reduce(gs[:, value, :], src, AX.X, ALU.max))
                    chain.link(dve.tensor_tensor(g3[6], src, bc(value), ALU.is_equal))
                    chain.link(dve.tensor_tensor(g3[6], g3[6], rank, ALU.mult))
                    chain.link(dve.tensor_reduce(gs[:, 4, :], g3[6], AX.X, ALU.max))
                    chain.link(dve.tensor_tensor(g3[onehot], bc(4), rank, ALU.is_equal))

                def softmax():
                    dve.wait_ge(ex_ready, n + 1)
                    chain.link(dve.tensor_reduce(gs[:, 1, :], g3[1], AX.X, ALU.add))
                    chain.link(dve.reciprocal(gs[:, 1, :], gs[:, 1, :]))
                    chain.link(dve.tensor_tensor(g3[2], g3[1], bc(1), ALU.mult))

                def largest():
                    top(g3[2], 2, 3)
                    chain.link(dve.scalar_tensor_tensor(out=g3[4], in0=g3[3], scalar=-2.0, in1=g3[2],
                                                        op0=ALU.mult, op1=ALU.add))

                def second():
                    top(g3[4], 3, 5)

                def weights():
                    dve.tensor_tensor(g3[3], g3[3], g3[5], ALU.add)
                    chain.link(dve.tensor_tensor(gs[:, 5, :], gs[:, 2, :], gs[:, 3, :], ALU.add))
                    chain.link(dve.reciprocal(gs[:, 5, :], gs[:, 5, :]))
                    chain.link(dve.tensor_tensor(g3[3], g3[3], g3[2], ALU.mult))
                    if not (isinstance(c, int) and c == 0 and layer == 0):
                        dve.wait_ge(w_turned, n)
                    dve.tensor_tensor(gate[:, 7, :].rearrange("p (e t) -> p t e", e=EXPERTS), g3[3], bc(5),
                                      ALU.mult).then_inc(w_ready, 1)

                def copy_w():
                    dve.wait_ge(w_turned, n + 1)
                    if not (isinstance(c, int) and c == 0 and layer == 0):
                        dve.wait_ge(w_written, n * 16)
                    dve.tensor_copy(wts_t, ps[0:32, bank, 0:128]).then_inc(wt_ready, 1)
                return recompute, residual, shift2, split_m, gate1, softmax, largest, second, weights, copy_w

            CHAIN_LINKS = 4 + 1 + 1 + 1 + (3 + 5 + 1 + 5 + 3)

            def expert(n, par, e, first):
                if e == 0:
                    dve.wait_ge(w_spread, n * 16 + 16)
                dve.wait_ge(down_done, n * 32 + (FB * e + FB))
                if e >= 2:
                    dve.wait_ge(tmp_added, n * 7 + max(e - 2, 1))
                elif not first:
                    dve.wait_ge(tmp_added, n * 7)
                dve.scalar_tensor_tensor(out=tmp[e % 2], in0=ps[:, 4 + e % 2, :], scalar=b2_sb[:, e:e + 1],
                                         in1=wbc[par][:, e * 512:(e + 1) * 512], op0=ALU.add,
                                         op1=ALU.mult).then_inc(tmp_ready, 1)

            def finish(layer, c):
                n = layer * CHUNKS + c
                dve.wait_ge(out_turned, n + 1)
                xs = x[:, bass.ds(c * 512, 512)]
                dve.scalar_tensor_tensor(out=xs, in0=ps[:, 7, :], scalar=0.5, in1=xs, op0=ALU.mult,
                                         op1=ALU.add).then_inc(x_final, 1)
                if layer == 0:
                    dve.wait_ge(x_final, n + 1)
                    dve.nop(nofuse=True)
                    for j in range(4):
                        tile_stats(c * 4 + j)

            def mix(layer):
                def one(c, par, before, after):
                    n = layer * CHUNKS + c
                    first = not before and layer == 0
                    parts = chain_parts(layer, c + 1, (par + 1) % 2) if after else None
                    at = dict(zip((3, 6, 8, 16, 18, 20, 22, 24, 25, 30), parts or ()))
                    for k in range(BLOCKS):
                        dve.wait_ge(gelu_done, n * 32 + (k + 1))
                        if k >= 8 or not first:
                            dve.wait_ge(down_done, n * 32 + (k - 7))
                        dve.tensor_copy(hp[0][k % 8], hr[k % 4]).then_inc(hh_ready, 1)
                        if k % 2:
                            dve.wait_ge(hh_ready, n * 32 + k)
                            dve.tensor_tensor(hp[1][(k - 1) % 8], hr[(k - 1) % 4],
                                              hp[0][(k - 1) % 8].bitcast(F32), ALU.subtract).then_inc(hl_even, 1)
                        e = expert_at(k)
                        if e is not None and e >= 0:
                            expert(n, par, e, first)
                        elif e is not None and before:
                            expert(n - 1, (par + 1) % 2, e + EXPERTS, False)
                        if k == 11 and before:
                            finish(layer, c - 1)
                        if k in at:
                            at[k]()
                one(0, 0, False, True)
                with dve.Fori(0, 3) as i:
                    chain.loop(i, 2 * CHAIN_LINKS)
                    one(i * 2 + 1, 1, True, True)
                    one(i * 2 + 2, 0, True, True)
                    chain.end(3, 2 * CHAIN_LINKS)
                one(CHUNKS - 1, 1, True, False)
                for e in (EXPERTS - 2, EXPERTS - 1):
                    expert((layer + 1) * CHUNKS - 1, 1, e, False)
                finish(layer, CHUNKS - 1)

            def retain():
                chain.link(dve.tensor_scalar(cols[:, 5:6], cols[:, 4:5], 0.0, None, ALU.mult))
                dve.tensor_copy(cols[:, 5:6], cols[:, 5:6]).then_inc(theta_z, 1)
                dve.wait_ge(x_final, CHUNKS)
                stats(1)
                dve.wait_ge(sd_ready, 3)
                chain.link(dve.reciprocal(rstd[:, :], sd[:, :]))
                dve.scalar_tensor_tensor(out=shift[:, :], in0=mean[:, :], scalar=-1.0, in1=rstd[:, :],
                                         op0=ALU.mult, op1=ALU.mult).then_inc(norm_ready, 1)
                dve.wait_ge(theta_e, 1)
                dve.tensor_tensor(cols[:, 7:8], cols[:, 6:7], cols[:, 6:7], ALU.mult).then_inc(theta_e, 1)
                b4 = "p (b n) -> p b n"

                def turned_z(c, u):
                    dve.wait_ge(rz_turned, c + 1)
                    dve.tensor_copy(rzt[u], ps[:, 7, :]).then_inc(rzt_ready, 1)

                def values(c, u):
                    dve.wait_ge(rkd_ready, c + 1)
                    dve.tensor_copy(rv[u].rearrange(b4, b=BATCH),
                                    ps[:, 2:4, :].rearrange("p a (b n) -> p (a b) n", b=2)[:, :, 0:D]
                                    ).then_inc(rv_ready, 1)

                def result(c):
                    dve.wait_ge(ro_done, c + 1)
                    xs = x[:, :].rearrange(b4, b=BATCH)[:, :, bass.ds(c * D, D)]
                    dve.tensor_tensor(xs, ps[:, 5, :].rearrange(b4, b=BATCH), xs, ALU.add).then_inc(rx_done, 1)

                def result_stats(c):
                    dve.wait_ge(rx_done, c + 1)
                    dve.nop(nofuse=True)
                    for b in range(BATCH):
                        tile_stats(c + b * KT)

                def step(c, u, first=False, last=False):
                    if not last:
                        turned_z(c + 1, 1 - u)
                    if not first:
                        result(c - 1)
                    dve.wait_ge(ra_done, c + 1)
                    dve.tensor_tensor(ram.rearrange(b4, b=BATCH), ps[:, 4, :].rearrange(b4, b=BATCH),
                                      tab[:, C_MASK:C_MASK + P].unsqueeze(1).broadcast_to([P, BATCH, P]),
                                      ALU.mult).then_inc(ram_ready, 1)
                    if not first:
                        dve.wait_ge(rst_done, c)
                        dve.scalar_tensor_tensor(out=state[:, :], in0=state[:, :], scalar=GAMMA ** P,
                                                 in1=ps[:, 6, :], op0=ALU.mult, op1=ALU.add
                                                 ).then_inc(state_ready, 1)
                    if not last:
                        values(c + 1, 1 - u)
                    if not first:
                        result_stats(c - 1)
                turned_z(0, 0)
                values(0, 0)
                step(0, 0, first=True)
                with dve.Fori(0, KT // 2 - 1) as i:
                    step(i * 2 + 1, 1)
                    step(i * 2 + 2, 0)
                step(KT - 1, 1, last=True)
                result(KT - 1)
                result_stats(KT - 1)

            for layer in range(2):
                project(layer)
                attend(layer)
                mix(layer)
                if layer == 0:
                    retain()

        @block.tensor
        def _(pe):
            mm = pe.matmul

            def turn4(bank, src):
                for j in range(4):
                    last = pe.transpose(ps[:, bank, j * P:(j + 1) * P], src[:, j * P:(j + 1) * P], ident)
                return last

            def project_turn(layer, c, bank):
                n = layer * CHUNKS + c
                pe.wait_ge(zn_ready, n + 1)
                turn4(bank, zn[c % 2]).then_inc(zn_turned, 1)

            def project_tile(layer, c, j, bank, ago):
                pe.wait_ge(ht_ready, layer * CHUNKS + c + 1)
                if layer or c * 4 + j >= ago:
                    pe.wait_ge(qkv_stored, layer * TILES + c * 4 + (j + 1 - ago))
                mm(ps[:, bank, 0:3 * D], ht[c % 2][:, j * P:(j + 1) * P], wqkv_sb[:, :], start=True,
                   stop=True).then_inc(qkv_done, 1)

            def project(layer):
                project_turn(layer, 0, 6)
                project_turn(layer, 1, 7)
                for c in range(EARLY):
                    for j in range(4):
                        if j == 3 and 1 <= c < EARLY - 1:
                            project_turn(layer, c + 1, 6 + (c + 1) % 2)
                        project_tile(layer, c, j, j, 4)

            def turn(layer, name, par, G, count, first):
                if not first:
                    pe.wait_ge(turn_taken, count)
                if name in ("ctx0", "ctx1"):
                    pe.wait_ge(ct_ready, G * 2 + (1 if name == "ctx0" else 0))
                    turn4(7, ct[:, :]).then_inc(turned, 1)
                    return
                if name in ("k_early", "q_early"):
                    pe.wait_ge(kst_ready if name == "k_early" else qst_ready, G + 3)
                if name == "qm_late":
                    pe.wait_ge(neg_ready, G * 2 + 2)
                if name == "qm_early":
                    pe.wait_ge(neg_ready, G * 2 + 3)
                src, half = {"k_late": (kst, 1), "k_early": (kst, 0), "q_late": (qst[(par + 1) % 2], 1),
                             "q_early": (qst[par], 0), "qm_late": (qst[par], 1),
                             "qm_early": (qst[(par + 1) % 2], 0)}[name]
                dst = ps[:, 7, :].bitcast(BF16).rearrange("p (a n) -> p a n", a=2)
                for pair in range(2):
                    for t in range(4):
                        last = pe.transpose(dst[:, pair, t * P:(t + 1) * P],
                                            src[:, 4 * half + t, 2 * pair:2 * pair + 2, :], ident_b[:, :])
                last.then_inc(turned, 1)

            def body(layer, g, par, n):
                G = g + layer * GROUPS
                at = {s: (name, i) for i, (name, s) in enumerate(turns(n))}
                before = takes_before(g) + layer * TAKES_OF_LAYER
                attends, takes_max = 0 <= n < GROUPS, 0 <= n + 1 < GROUPS
                aside = dict(zip((2, 4, 8, 10, 14), chain_parts(layer, 0))) if n == GROUPS - 1 else {}
                projects = projections(n)
                banks, ago = ((0, 1, 4, 5), 4) if n == GROUPS - 1 else ((0, 1, 0, 1), 2)
                if n == 0:
                    pe.wait_ge(qkv_stored, (layer + 1) * TILES)

                def score(s, u):
                    if n or s or u > 1 or layer:
                        pe.wait_ge(exp_done, G * 64 + (4 * s + u + 1 - (ago if s else 2)))
                    if n == GROUPS - 1 and s == 0 and u == 2:
                        pe.wait_ge(max_taken, (layer + 1) * GROUPS * 64)
                    mm(ps[:, banks[u], :], kpad[par][:, u, s % 8 * P:(s % 8 + 1) * P], qm[s // 8][:, u // 2, :],
                       start=True, stop=True).then_inc(s_filled, 1)

                def top(s, u):
                    half, kh, j = s // 8, s % 8 // 4, s % 4
                    if n >= 0 or s or layer:
                        pe.wait_ge(max_taken, G * 64 + (64 + 4 * s + u - 3))
                    mm(ps[:, 2 + u, :], q0[half][:, u // 2, j * P:(j + 1) * P],
                       kpad[(par + 1) % 2][:, u, kh * 512:kh * 512 + 512], start=True,
                       stop=True).then_inc(max_filled, 1)

                def weigh(s, G, par):
                    pe.wait_ge(exp_done, G * 64 + (4 * s + 4))
                    if s == 0:
                        pe.wait_ge(vst_ready, G + 1)
                    if s % 8 == 0 and (s or n or layer):
                        pe.wait_ge(ct_ready, G * 2 + s // 8)
                    for u in range(GH):
                        last = mm(ps[32 * u:32 * u + 32, 6, :], vst[par][:, s % 8, u, :], pbuf[:, s % 2, u, :],
                                  start=(s % 8 == 0), stop=(s % 8 == 7))
                    last.then_inc(pv_done, 1)

                for s in range(16 if n < GROUPS else 3):
                    if s in aside:
                        aside[s]()
                    if s in at:
                        turn(layer, at[s][0], par, G, before + (takes_upto(n, at[s][0]) - takes(at[s][0])),
                             n == -2 and at[s][1] == 0 and not layer)
                    if s == 0 and n > -2 and n < GROUPS:
                        pe.wait_ge(turn_taken, before)
                    if s == 4 and takes_max:
                        pe.wait_ge(turn_taken, before + takes_upto(n, "k_late"))
                    if s == 8 and takes_max:
                        pe.wait_ge(turn_taken, before + takes_upto(n, "q_late"))
                    if s == 8 and attends:
                        pe.wait_ge(turn_taken, before + takes_upto(n, "qm_late"))
                    order = ("s0", "m0", "s1", "m1", "m2", "s2", "m3", "s3")
                    for what in order:
                        if what[0] == "s" and attends:
                            score(s, int(what[1]))
                        if what[0] == "m" and takes_max:
                            top(s, int(what[1]))
                    if s == 0:
                        if n >= 1:
                            weigh(15, G - 1, (par + 1) % 2)
                    elif attends:
                        weigh(s - 1, G, par)
                    for what, c, j in projects[s]:
                        if what == "turn":
                            project_turn(layer, c, 6)
                        else:
                            project_tile(layer, c, j, j % 2, 2)

            def chain_parts(layer, c):
                n = layer * CHUNKS + c
                first = isinstance(c, int) and c == 0
                bank, products = chain_banks(c)

                def turn_cx():
                    pe.wait_ge(cbuf_ready, n + 1)
                    if isinstance(c, int) and c == 1:
                        pe.wait_ge(turn_taken, (layer + 1) * TAKES_OF_LAYER)
                    elif first:
                        pe.wait_ge(max_taken, (layer + 1) * GROUPS * 64)
                    else:
                        pe.wait_ge(wt_ready, n)
                    turn4(bank, cbuf).then_inc(cx_turned, 1)

                def project_out():
                    pe.wait_ge(cxt_ready, n + 1)
                    if not first:
                        pe.wait_ge(lm_ready, n)
                    for j in range(4):
                        last = mm(ps[:, products, j * P:(j + 1) * P], cxt[:, j * P:(j + 1) * P], wo_sb[:, :],
                                  start=True, stop=True)
                    last.then_inc(wo_done, 1)

                def turn_zn2():
                    pe.wait_ge(zn2_ready, n + 1)
                    if not isinstance(c, int):
                        pe.wait_ge(x_final, n - 1)
                    turn4(bank, zn2).then_inc(zn2_turned, 1)

                def logits():
                    pe.wait_ge(mtf_ready, n + 1)
                    for j in range(4):
                        last = mm(ps[:, products, j * EXPERTS:(j + 1) * EXPERTS], mtf[:, j * P:(j + 1) * P],
                                  wg_sb[:, :], start=True, stop=True)
                    last.then_inc(logits_done, 1)

                def turn_w():
                    pe.wait_ge(w_ready, n + 1)
                    pe.transpose(ps[0:32, bank, 0:P], gate[:, 7, :], ident).then_inc(w_turned, 1)
                return turn_cx, project_out, turn_zn2, logits, turn_w

            def turn_out(layer, c):
                n = layer * CHUNKS + c
                pe.wait_ge(tmp_added, n * 7 + 7)
                if isinstance(c, int) and c == CHUNKS - 1:
                    pe.wait_ge(x_final, n)
                elif isinstance(c, int) and c == CHUNKS - 2:
                    pe.wait_ge(wt_ready, n + 2)
                else:
                    pe.wait_ge(cxt_ready, n + 3)
                turn4(7, acc).then_inc(out_turned, 1)

            def experts(layer, c, par, at):
                n = layer * CHUNKS + c
                w1v = [half.rearrange("p (e f) -> p e f", e=EXPERTS) for half in w1p]

                def hidden(k):
                    if k == 0:
                        pe.wait_ge(mt_ready, n + 1)
                    if k in (2, 3) and isinstance(c, int) and c == 0:
                        pe.wait_ge((wt_ready, lm_ready)[k - 2], n + 1)
                    if k >= 4 or not (isinstance(c, int) and c == 0 and layer == 0):
                        pe.wait_ge(gelu_done, n * 32 + (k - 3))
                    if k == 0 and layer == 0 and isinstance(c, int) and c == 0:
                        pe.wait_ge(w_rest, W_PIECES)
                    cut = slice(k % FB * P, (k % FB + 1) * P)
                    for i, (a, b) in enumerate(((0, 0), (0, 1), (1, 0))):
                        last = mm(ps[:, k % 4, :], w1v[a][:, k // FB, cut], mtp[b][par], start=(i == 0),
                                  stop=(i == 2))
                    last.then_inc(h_filled, 1)

                for k in range(BLOCKS):
                    for f in at.get(k, ()):
                        f()
                    hidden(k)
                    if k >= LAG:
                        down(n, k - LAG, isinstance(c, int) and c == 0 and layer == 0)
                    elif not (isinstance(c, int) and c == 0):
                        down(n - 1, BLOCKS - LAG + k, False)

            def down(n, k, first):
                e, f = k // FB, k % FB
                pe.wait_ge(hh_ready, n * 32 + (k + 1))
                pe.wait_ge(hl_odd if k % 2 else hl_even, n * 16 + (k // 2 + 1))
                if f == 0 and not (first and e < 2):
                    pe.wait_ge(tmp_ready, n * 8 + (e - 1))
                w2v = [half.rearrange("p (e f d) -> p e f d", e=EXPERTS, f=FB) for half in w2p]
                for i, (a, b) in enumerate(((0, 0), (0, 1), (1, 0))):
                    last = mm(ps[:, 4 + e % 2, :], w2v[a][:, e, f, :], hp[b][k % 8], start=(f == 0 and i == 0),
                              stop=(f == FB - 1 and i == 2))
                last.then_inc(down_done, 1)

            def mix(layer):
                def one(c, par, before):
                    parts = chain_parts(layer, c + 1)
                    at = {2: (parts[0],), 5: (parts[1],), 15: (parts[2],), 18: (parts[3],), 31: (parts[4],)}
                    if before:
                        at[10] = (lambda: turn_out(layer, c - 1),)
                    experts(layer, c, par, at)
                one(0, 0, False)
                with pe.Fori(0, 3) as i:
                    one(i * 2 + 1, 1, True)
                    one(i * 2 + 2, 0, True)
                experts(layer, CHUNKS - 1, 1, {10: (lambda: turn_out(layer, CHUNKS - 2),)})
                for k in range(BLOCKS - LAG, BLOCKS):
                    down((layer + 1) * CHUNKS - 1, k, False)
                turn_out(layer, CHUNKS - 1)

            def retain():
                pe.wait_ge(x_final, CHUNKS)

                def turn_z(c, u, first=False):
                    pe.wait_ge(rz_ready, c + 1)
                    if not first:
                        pe.wait_ge(rzt_ready, c)
                    turn4(7, zn[u]).then_inc(rz_turned, 1)

                def products(c, u):
                    pe.wait_ge(rzt_ready, c + 1)
                    mm(ps[:, 0, :], rw_sb[:, 0:D], rzt[u], start=True, stop=True).then_inc(rq_done, 1)
                    mm(ps[:, 1, :], rw_sb[:, D:2 * D], rzt[u], start=True, stop=True).then_inc(rk_done, 1)
                    for b in range(BATCH):
                        last = mm(ps[:, 2 + b // 2, b % 2 * 256:b % 2 * 256 + 256], rzt[u][:, b * P:(b + 1) * P],
                                  rw_sb[:, 2 * D:4 * D], start=True, stop=True)
                    last.then_inc(rkv_done, 1)

                def step(c, u, first=False, last=False):
                    if not last:
                        turn_z(c + 1, 1 - u)
                    cuts = [slice(b * P, (b + 1) * P) for b in range(BATCH)]
                    pe.wait_ge(rq_ready, c + 1)
                    pe.wait_ge(rk_ready, c + 1)
                    if not first:
                        pe.wait_ge(ram_ready, c)
                    for cut in cuts:
                        end = mm(ps[:, 4, cut], rk[u][:, cut], rq[u][:, cut], start=True, stop=True)
                    end.then_inc(ra_done, 1)
                    pe.wait_ge(rkd_ready, c + 1)
                    pe.wait_ge(rv_ready, c + 1)
                    if not last:
                        products(c + 1, 1 - u)
                    if not first:
                        pe.wait_ge(state_ready, c)
                    if not last:
                        for cut in cuts:
                            end = mm(ps[:, 6, cut], rkd[u][:, cut], rv[u][:, cut], start=True, stop=True)
                        end.then_inc(rst_done, 1)
                    pe.wait_ge(ram_ready, c + 1)
                    pe.wait_ge(rqd_ready, c + 1)
                    if not first:
                        pe.wait_ge(rx_done, c)
                    for cut in cuts:
                        mm(ps[:, 5, cut], ram[:, cut], rv[u][:, cut], start=True, stop=False)
                        end = mm(ps[:, 5, cut], rqd[u][:, cut], state[:, cut], start=False, stop=True)
                    end.then_inc(ro_done, 1)
                turn_z(0, 0, first=True)
                products(0, 0)
                step(0, 0, first=True)
                with pe.Fori(0, KT // 2 - 1) as i:
                    step(i * 2 + 1, 1)
                    step(i * 2 + 2, 0)
                step(KT - 1, 1, last=True)

            pe.wait_ge(consts_done, 1)
            for layer in range(2):
                project(layer)
                bodies(pe, lambda g, par, n: body(layer, g, par, n))
                mix(layer)
                if layer == 0:
                    retain()


def constants():
    import numpy as np
    i = np.arange(P, dtype=np.float64)
    t = np.zeros((P, C_END), np.float32)
    t[:, C_IDENT:C_IDENT + P] = np.eye(P)
    diff = i[None, :] - i[:, None]
    t[:, C_MASK:C_MASK + P] = np.where(diff >= 0, GAMMA ** np.maximum(diff, 0), 0.0)
    t[:, C_ROW:C_ROW + P] = GAMMA ** (i + 1)[None, :]
    t[:, C_COL] = GAMMA ** (P - 1 - i)
    t[:, C_RANK:C_RANK + EXPERTS] = EXPERTS - np.arange(EXPERTS)
    return t


def laid_out(L0_attn_x, L0_attn_weight_q, L0_attn_weight_k, L0_attn_weight_v, L0_attn_theta, L0_ffn_ln1_g,
             L0_ffn_ln1_b, L0_ffn_ln2_g, L0_ffn_ln2_b, L0_ffn_Wq, L0_ffn_Wk, L0_ffn_Wv, L0_ffn_Wo, L0_ffn_Wg,
             L0_ffn_W1, L0_ffn_b1, L0_ffn_W2, L0_ffn_b2):
    import numpy as np
    vectors = (L0_ffn_ln1_g, L0_ffn_ln1_b, L0_ffn_ln2_g, L0_ffn_ln2_b, L0_attn_theta)
    room = np.zeros((D, 3), np.float32)
    small = {"table": constants(), "cols": np.concatenate([np.stack(vectors, 1), room], 1),
             "wqkv": np.concatenate([L0_ffn_Wq, L0_ffn_Wk, L0_ffn_Wv], 1), "wo": L0_ffn_Wo, "wg": L0_ffn_Wg,
             "rw": np.concatenate([L0_attn_weight_q, L0_attn_weight_k, L0_attn_weight_v, L0_attn_weight_k], 1),
             "b1": L0_ffn_b1.reshape(EXPERTS * FB, P).T, "b2": L0_ffn_b2.T}
    return {"x": L0_attn_x.reshape(TILES, P, D).transpose(1, 0, 2).reshape(P, TILES * D),
            "small": np.concatenate([small[name] for name, _ in SMALL], 1),
            "w": np.concatenate([L0_ffn_W1.transpose(1, 0, 2).reshape(P, EXPERTS * FF),
                                 L0_ffn_W2.reshape(EXPERTS, FB, P, D).transpose(2, 0, 1, 3)
                                 .reshape(P, BLOCKS * D)], 1)}


def kernel(**inputs):
    import numpy as np
    import concourse.bacc as bacc
    from concourse.bass_utils import run_bass_kernel_spmd

    nc = bacc.Bacc("TRN2", target_bir_lowering=False, num_devices=1)
    arrays = laid_out(**{name: np.asarray(a) for name, a in inputs.items()})
    arrays = {name: np.ascontiguousarray(a) for name, a in arrays.items()}
    args = [nc.dram_tensor(f"in_{name}", a.shape, mybir.dt.from_np(a.dtype), kind="ExternalInput").ap()
            for name, a in arrays.items()]
    out = nc.dram_tensor("result", (P, TILES * D), F32, kind="ExternalOutput").ap()
    macaron(nc, *args, out)
    r = run_bass_kernel_spmd(nc, [{f"in_{name}": a for name, a in arrays.items()}], core_ids=[0])
    return r.results[0]["result"].reshape(P, TILES, D).transpose(1, 0, 2).reshape(BATCH, SEQ, D)
```
